# Optimizing a Trainium2 kernel written in Bass

```python
import numpy as np
import jax
import jax.numpy as jnp

def _softmax(x, axis=-1):
    return jax.nn.softmax(x, axis=axis)
def _gelu(x):
    return jax.nn.gelu(x, approximate=True)
def _silu(x):
    return jax.nn.silu(x)
def _sigmoid(x):
    return jax.nn.sigmoid(x)
def _layernorm(x, axis=-1, eps=1e-5):
    m = jnp.mean(x, axis=axis, keepdims=True)
    v = jnp.var(x, axis=axis, keepdims=True)
    return (x - m) / jnp.sqrt(v + eps)
def _scatter_add(tgt, idx, src, axis=0):
    return tgt.at[idx].add(src)
def _segment_sum(src, seg, n):
    return jax.ops.segment_sum(src, seg, n)

kernel_name = 'mk_conv_seq_d1_conv_nchw64_9110ba'

def setup_inputs(seed: int = 0):
    np.random.seed(seed)
    _w = jnp.asarray
    def _rec_inputs():
        import jax
        import jax.numpy as jnp
        _gk = jax.random.key(seed)
        x = -7.109e-05 + 0.9999 * jax.random.normal(jax.random.fold_in(_gk, 1), (16, 64, 256, 256), jnp.float32)
        return x
    x = _rec_inputs()
    def _L0_conv_setup():
        import jax, jax.numpy as jnp
        import numpy as np
        B, C, H, W = (16, 64, 256, 256)
        MX, MY = (16, 16)
        GROUPS = 32
        EPS = 1e-05

        def _fno_layer(x, w1_re, w1_im, w2_re, w2_im, conv_w, conv_b, gn_w, gn_b):
            w1 = w1_re + 1j * w1_im
            w2 = w2_re + 1j * w2_im
            x_ft = jnp.fft.rfft2(x, axes=(-2, -1))
            top = jnp.einsum('bixy,ioxy->boxy', x_ft[:, :, :MX, :MY], w1)
            bot = jnp.einsum('bixy,ioxy->boxy', x_ft[:, :, H - MX:, :MY], w2)
            out_ft = jnp.zeros((B, C, H, W // 2 + 1), dtype=x_ft.dtype)
            out_ft = out_ft.at[:, :, :MX, :MY].set(top)
            out_ft = out_ft.at[:, :, H - MX:, :MY].set(bot)
            x_spec = jnp.fft.irfft2(out_ft, s=(H, W), axes=(-2, -1))
            x_loc = jnp.einsum('oi,bixy->boxy', conv_w, x) + conv_b[None, :, None, None]
            h = jax.nn.gelu(x_spec + x_loc + x, approximate=False)
            g = h.reshape(B, GROUPS, C // GROUPS, H, W)
            mu = g.mean(axis=(2, 3, 4), keepdims=True)
            var = g.var(axis=(2, 3, 4), keepdims=True)
            g = (g - mu) / jnp.sqrt(var + EPS)
            h = g.reshape(B, C, H, W)
            return h * gn_w[None, :, None, None] + gn_b[None, :, None, None]
        key = jax.random.key(seed)
        ks = jax.random.split(key, 9)
        scale = 1.0 / (C * C)
        f = lambda k, sh: jax.random.normal(k, sh, dtype=jnp.float32)
        return {'x': f(ks[0], (B, C, H, W)), 'w1_re': f(ks[1], (C, C, MX, MY)) * scale, 'w1_im': f(ks[2], (C, C, MX, MY)) * scale, 'w2_re': f(ks[3], (C, C, MX, MY)) * scale, 'w2_im': f(ks[4], (C, C, MX, MY)) * scale, 'conv_w': f(ks[5], (C, C)) * (1.0 / np.sqrt(C)), 'conv_b': f(ks[6], (C,)) * 0.01, 'gn_w': jnp.ones((C,), jnp.float32), 'gn_b': jnp.zeros((C,), jnp.float32)}
    _L0_conv_all = _L0_conv_setup()
    _L0_conv_in = {k: v for k, v in _L0_conv_all.items() if k in ('w1_re', 'w1_im', 'w2_re', 'w2_im', 'conv_w', 'conv_b', 'gn_w', 'gn_b', )}
    del _L0_conv_all

    return {
        "x": x,
        "L0_conv_w1_re": _L0_conv_in["w1_re"],
        "L0_conv_w1_im": _L0_conv_in["w1_im"],
        "L0_conv_w2_re": _L0_conv_in["w2_re"],
        "L0_conv_w2_im": _L0_conv_in["w2_im"],
        "L0_conv_conv_w": _L0_conv_in["conv_w"],
        "L0_conv_conv_b": _L0_conv_in["conv_b"],
        "L0_conv_gn_w": _L0_conv_in["gn_w"],
        "L0_conv_gn_b": _L0_conv_in["gn_b"],
    }

def reference(x, L0_conv_w1_re, L0_conv_w1_im, L0_conv_w2_re, L0_conv_w2_im, L0_conv_conv_w, L0_conv_conv_b, L0_conv_gn_w, L0_conv_gn_b):
    import jax
    import jax.numpy as jnp
    def _L0_conv_ref(x, w1_re, w1_im, w2_re, w2_im, conv_w, conv_b, gn_w, gn_b):
        import jax, jax.numpy as jnp
        import numpy as np
        B, C, H, W = (16, 64, 256, 256)
        MX, MY = (16, 16)
        GROUPS = 32
        EPS = 1e-05

        def _fno_layer(x, w1_re, w1_im, w2_re, w2_im, conv_w, conv_b, gn_w, gn_b):
            w1 = w1_re + 1j * w1_im
            w2 = w2_re + 1j * w2_im
            x_ft = jnp.fft.rfft2(x, axes=(-2, -1))
            top = jnp.einsum('bixy,ioxy->boxy', x_ft[:, :, :MX, :MY], w1)
            bot = jnp.einsum('bixy,ioxy->boxy', x_ft[:, :, H - MX:, :MY], w2)
            out_ft = jnp.zeros((B, C, H, W // 2 + 1), dtype=x_ft.dtype)
            out_ft = out_ft.at[:, :, :MX, :MY].set(top)
            out_ft = out_ft.at[:, :, H - MX:, :MY].set(bot)
            x_spec = jnp.fft.irfft2(out_ft, s=(H, W), axes=(-2, -1))
            x_loc = jnp.einsum('oi,bixy->boxy', conv_w, x) + conv_b[None, :, None, None]
            h = jax.nn.gelu(x_spec + x_loc + x, approximate=False)
            g = h.reshape(B, GROUPS, C // GROUPS, H, W)
            mu = g.mean(axis=(2, 3, 4), keepdims=True)
            var = g.var(axis=(2, 3, 4), keepdims=True)
            g = (g - mu) / jnp.sqrt(var + EPS)
            h = g.reshape(B, C, H, W)
            return h * gn_w[None, :, None, None] + gn_b[None, :, None, None]
        return _fno_layer(x, w1_re, w1_im, w2_re, w2_im, conv_w, conv_b, gn_w, gn_b)

    def _gn(v, G=32, eps=1e-5):
        B_, C_, H_, W_ = v.shape
        g = v.reshape(B_, G, C_ // G, H_, W_)
        m = jnp.mean(g, axis=(2, 3, 4), keepdims=True)
        s = jnp.var(g, axis=(2, 3, 4), keepdims=True)
        return ((g - m) / jnp.sqrt(s + eps)).reshape(v.shape)

    def _ln_c(v, eps=1e-6):
        m = jnp.mean(v, axis=1, keepdims=True)
        s = jnp.var(v, axis=1, keepdims=True)
        return (v - m) / jnp.sqrt(s + eps)

    def _ln_t(v, eps=1e-5):
        m = jnp.mean(v, axis=-1, keepdims=True)
        s = jnp.var(v, axis=-1, keepdims=True)
        return (v - m) / jnp.sqrt(s + eps)

    def _to_tokens(v):
        B_, C_, H_, W_ = v.shape
        return v.reshape(B_, C_, H_ * W_).transpose(0, 2, 1)
    def _from_tokens(t, like):
        B_, C_, H_, W_ = like.shape
        return t.transpose(0, 2, 1).reshape(B_, C_, H_, W_)

    x = _L0_conv_ref(x, L0_conv_w1_re, L0_conv_w1_im, L0_conv_w2_re, L0_conv_w2_im, L0_conv_conv_w, L0_conv_conv_b, L0_conv_gn_w, L0_conv_gn_b)
    return x


_drawn_inputs = setup_inputs


def setup_inputs(seed=0):
    import zlib

    import numpy as np

    out = dict(_drawn_inputs(seed))
    spreads = {'L0_conv_gn_w': (1.0, 0.2), 'L0_conv_gn_b': (0.0, 0.1)}
    factors = {'L0_conv_w1_re': 200.0,
     'L0_conv_w1_im': 200.0,
     'L0_conv_w2_re': 200.0,
     'L0_conv_w2_im': 200.0,
     'L0_conv_conv_b': 7.564}
    for name, (base, spread) in spreads.items():
        noise = np.random.default_rng([zlib.crc32(name.encode()), seed]).standard_normal(out[name].shape)
        drawn = base * np.exp(spread * noise) if base else spread * noise
        out[name] = jnp.asarray(drawn.astype(out[name].dtype))
    for name, factor in factors.items():
        out[name] = (out[name] * factor).astype(out[name].dtype)
    return out
```

```python
from contextlib import ExitStack

import numpy as np

import concourse.bass as bass
from concourse import mybir

F32 = mybir.dt.float32
F32R = mybir.dt.float32r
ALU = mybir.AluOpType
ACT = mybir.ActivationFunctionType

B, C, H, W = 16, 64, 256, 256
MX, MY = 16, 16
GROUPS = 32
EPS = 1e-5
P = 128
HH = H // 2
KH = MX + 1
KC = KH + MX
SLOTS = 2 * MX
RI = 2
MODE = 2 * B

CH = 4
NX = 4
TILE = 2048
A_TILES = C // CH

WX = 4
NW = 3
W_CHUNKS = 2 * MX // WX

TILES = HH * W // TILE
GRP = 1024
BANK = 512
GROUPS_B = HH * W // GRP
SL = 4
SL_ROWS = HH // SL
SL_TILES = TILES // SL
JJ = 4
QC = 4
QO = C // QC

CONST_COLS = {
    "dft_h": 2 * KC, "dft_w": 2 * 2 * 64, "idft_h": 256, "idft_w": 256, "group": P,
    "dup": P, "same_half": P, "ident": P, "sign": 1, "neg_half": 1,
}


def top12(a):
    u = np.asarray(a, np.float32).view(np.uint32).astype(np.uint64)
    u = (u + 0x7FF + ((u >> 12) & 1)) & 0xFFFFF000
    return u.astype(np.uint32).view(np.float32)


def at_start(n):
    return isinstance(n, int) and n <= 0


def constants():
    c = {}
    p = np.arange(P)
    k = np.arange(KH)
    dft_h = np.zeros((P, 2, KC))
    for r in range(2):
        angle = 2 * np.pi * ((2 * p + r)[:, None] * k[None, :] % H) / H
        dft_h[:, r, :KH] = np.cos(angle)
        dft_h[:, r, KH:] = np.sin(angle)[:, 1:]
    c["dft_h"] = dft_h
    dft_w = np.zeros((P, 2, 2, 2, RI, MY))
    for chunk in range(2):
        angle = 2 * np.pi * ((P * chunk + p)[:, None] * np.arange(MY)[None, :] % W) / W
        cos, sin = np.cos(angle), np.sin(angle)
        for sign, s in ((0, 1), (1, -1)):
            dft_w[:, chunk, 0, sign, 0] = cos
            dft_w[:, chunk, 0, sign, 1] = -sin
            dft_w[:, chunk, 1, sign, 0] = -s * sin
            dft_w[:, chunk, 1, sign, 1] = -s * cos
    c["dft_w"] = dft_w
    kh = np.concatenate([np.arange(MX), -1 - np.arange(MX)])
    h = (np.arange(HH)[:, None] + HH * np.arange(2)[None, :]).ravel()
    angle = 2 * np.pi * (kh[:, None] * h[None, :] % H) / H
    c["idft_h"] = np.concatenate([np.cos(angle), -np.sin(angle)])
    angle = 2 * np.pi * (np.arange(MY)[:, None] * np.arange(W)[None, :] % W) / W
    twice = np.where(np.arange(MY) > 0, 2.0, 1.0)[:, None] / (H * W)
    e = np.concatenate([twice * np.cos(angle), -twice * np.sin(angle)]).astype(np.float32)
    high = top12(e)
    low = top12(e - high)
    c["idft_w"] = np.concatenate([high, low, high, low])
    span = 2 * C // GROUPS
    c["group"] = (p[:, None] // span == p[None, :] // span) / span
    c["dup"] = np.zeros((P, P))
    c["dup"][:C] = np.arange(C)[:, None] == p[None, :] // 2
    c["same_half"] = p[:, None] % 2 == p[None, :] % 2
    c["ident"] = np.eye(P)
    c["sign"] = np.where(p < SLOTS, 1.0, -1.0)
    c["neg_half"] = np.full(P, -0.5)
    return np.concatenate([np.asarray(c[n], np.float32).reshape(P, -1) if c[n].shape[0] == P else
                           np.pad(np.asarray(c[n], np.float32), ((0, P - c[n].shape[0]), (0, 0)))
                           for n in CONST_COLS], axis=1)


def fno_layer(nc, x, w1_re, w1_im, w2_re, w2_im, conv_w, conv_b, gn_w, gn_b, const, out):
    ctx = ExitStack()
    with ctx:
        def sb(name, shape, dt=F32, stack=ctx):
            return stack.enter_context(nc.sbuf_tensor(name, shape, dt))

        def psum(name, shape):
            return ctx.enter_context(nc.psum_tensor(name, shape, F32))

        def sem(name):
            return ctx.enter_context(nc.semaphore(name))

        xs = [sb(f"x_tile{i}", [P, TILE]) for i in range(2)]
        idft_h = sb("idft_h", [P, 256])
        idft_w = sb("idft_w", [P, 256], F32R)
        group = sb("group", [P, P])
        mix = sb("mix", [P, P])
        params = sb("params", [P, 3])
        signs = sb("signs", [P, 2])

        early = ExitStack()
        xa = xs + [sb(f"x_tile{i}", [P, TILE], stack=early) for i in range(2, NX)]
        xb = [xs[i // 2][:, i % 2 * GRP:(i % 2 + 1) * GRP] for i in range(NX)]
        dft_h = sb("dft_h", [P, 2, KC], stack=early)
        dft_w = sb("dft_w", [P, 2, 2, 64], stack=early)
        sums = sb("sums", [P, 2, KC, C], stack=early)
        spec = sb("spec", [P, SLOTS, MY, MODE], stack=early)
        wts = [sb(f"weights{i}", [P, C, WX * MY], stack=early) for i in range(NW)]
        mixed = [sb(f"mixed{i}", [MODE, WX, C * MY], stack=early) for i in range(2)]
        once = wts[NW - 1][:].rearrange("p a b -> p (a b)")
        dup = once[:, 0:P]
        same_half = once[:, P:2 * P]
        ident = once[:, 2 * P:3 * P]
        idft_w_raw = once[:, 3 * P:5 * P]
        cw = once[0:C, 5 * P:5 * P + C]
        cw2 = once[0:C, 6 * P:7 * P]
        prm = once[0:C, 7 * P:7 * P + 3]
        prod = once[:, 8 * P:9 * P]
        early.close()

        home = sb("home", [P, TILES, TILE])
        rows = [sb(f"row_modes{i}", [P, SL_ROWS, P], F32R) for i in range(2)]
        raw = sb("raw_modes", [C, RI, QO * MY])
        modes = sb("modes", [C, C, 2, RI * MY])
        stats = sb("stats", [P, TILES * 4, 6])
        small = sb("small", [P, 12])
        mean_var, dev, spread = small[:, 0:2], small[:, 2:3], small[:, 3:4]
        var_eps, rstd, scale, shift0, shift = (small[:, i:i + 1] for i in range(4, 9))
        gmean = small[:, 9:10]

        scratch = nc.dram_tensor("mixed_modes", [RI * B, SLOTS, C * MY], F32).ap()

        ps_main = psum("ps_main", [P, 4, BANK])
        ps_slice = psum("ps_slice", [P, 2, BANK])
        ps_small = psum("ps_small", [P, BANK])

        const_in = sem("const_in")
        cw_ready = sem("cw_ready")
        setup_mm = sem("setup_mm")
        mask_done = sem("mask_done")
        setup_done = sem("setup_done")
        x_in = [sem(f"x_in{i}") for i in range(NX)]
        xb_in = [sem(f"xb_in{i}") for i in range(NX)]
        w_in = [sem(f"w_in{i}") for i in range(NW)]
        a_sums = sem("a_sums")
        a_copied = sem("a_copied")
        a_modes = sem("a_modes")
        a_kept = sem("a_kept")
        m_mixed = sem("m_mixed")
        m_even = sem("m_even")
        m_odd = sem("m_odd")
        m_out = [sem(f"m_out{i}") for i in range(2)]
        raw_in = sem("raw_in")
        permuted = sem("permuted")
        kh_done = sem("kh_done")
        high = sem("high")
        low = sem("low")
        pre = sem("pre")
        gelu = sem("gelu")
        bn = sem("bn")
        bn_all = sem("bn_all")
        quarter_in = sem("quarter_in")
        chain = sem("chain")
        scaled = sem("scaled")
        gm_done = sem("gm_done")
        rstd_done = sem("rstd_done")
        normed = sem("normed")
        stored = [sem(f"stored{i}") for i in range(TILES)]

        x_a = x.rearrange("b c (p r) w -> p (b c) (r w)", r=2)
        x_b = x.rearrange("b c h w -> b (c h w)").rearrange("b (p n) -> p b n", p=P)
        out_b = out.rearrange("b c h w -> b (c h w)").rearrange("b (p n) -> p b n", p=P)
        col = {}
        at = 0
        for n, k in CONST_COLS.items():
            col[n] = const[:, at:at + k]
            at += k

        n_const = 13
        block = ctx.enter_context(nc.Block())

        @block.sync
        def _(sp):
            sp.dma_start(dft_h[:].rearrange("p a b -> p (a b)"), col["dft_h"]).then_inc(const_in, 16)
            sp.dma_start(dft_w[:].rearrange("p a b c -> p (a b c)"), col["dft_w"]).then_inc(const_in, 16)
            for s in range(NX):
                sp.dma_start(xa[s][:].rearrange("p (c n) -> p c n", c=CH),
                             x_a[:, s * CH:(s + 1) * CH, :]).then_inc(x_in[s], 16)
            sp.dma_start(idft_h[:], col["idft_h"]).then_inc(const_in, 16)
            sp.dma_start(idft_w_raw, col["idft_w"]).then_inc(const_in, 16)
            sp.dma_start(group[:], col["group"]).then_inc(const_in, 16)
            sp.dma_start(dup, col["dup"]).then_inc(const_in, 16)
            sp.dma_start(same_half, col["same_half"]).then_inc(const_in, 16)
            sp.dma_start(ident, col["ident"]).then_inc(const_in, 16)
            sp.dma_start(signs[:], const[:, at - 2:at]).then_inc(const_in, 16)
            sp.dma_start(cw, conv_w).then_inc(const_in, 16)
            for i, v in enumerate((conv_b, gn_w, gn_b)):
                sp.dma_start(prm[:, i:i + 1], v.rearrange("(c a) -> c a", a=1)).then_inc(const_in, 16)

            def weights(j):
                xx = WX * (j % (W_CHUNKS // 2))
                re, im = (w1_re, w1_im) if j < W_CHUNKS // 2 else (w2_re, w2_im)
                for half, w in ((0, re), (1, im)):
                    sp.dma_start(wts[j % NW][half * C:(half + 1) * C],
                                 w[:, :, xx:xx + WX, :].rearrange("i o x y -> i o (x y)")
                                 ).then_inc(w_in[j % NW], 16)

            sp.wait_ge(setup_done, 5)
            for j in range(NW):
                weights(j)
            with sp.Fori(1, B * A_TILES // NX) as u:
                for s in range(NX):
                    sp.wait_ge(a_sums, (u - 1) * NX + s + 1)
                    sp.dma_start(xa[s][:].rearrange("p (c n) -> p c n", c=CH),
                                 x_a[:, bass.ds((u * NX + s) * CH, CH), :]).then_inc(x_in[s], 16)

            def fetch(b, g):
                sp.dma_start(xb[g % NX], x_b[:, bass.ds(b, 1), g * GRP:(g + 1) * GRP]
                             .rearrange("p a n -> p (a n)")).then_inc(xb_in[g % NX], 16)

            sp.wait_ge(a_sums, B * A_TILES - NX + 2)
            for g in range(NX):
                fetch(0, g)
            for j in range(W_CHUNKS):
                if j + NW < W_CHUNKS:
                    sp.wait_ge(m_mixed, (j + 1) * 8)
                    weights(j + NW)
                sp.wait_ge(m_even, (j + 1) * 4)
                sp.wait_ge(m_odd, (j + 1) * 4)
                first = WX * j if j < W_CHUNKS // 2 else SLOTS - WX * (j - W_CHUNKS // 2 + 1)
                sp.dma_start(scratch[:, first:first + WX, :], mixed[j % 2][:]).then_inc(m_out[j % 2], 16)

            def load(b, g):
                sp.wait_ge(pre, GROUPS_B * b + g - NX + 1)
                fetch(b, g)

            def store(b, t):
                sp.wait_ge(normed, TILES * b + t + 1)
                sp.dma_start(out_b[:, bass.ds(b, 1), t * TILE:(t + 1) * TILE]
                             .rearrange("p a n -> p (a n)"), home[:, t, :]).then_inc(stored[t], 16)

            for g in range(NX, GROUPS_B):
                load(0, g)
            with sp.Fori(0, B - 1) as b:
                for g in range(NX):
                    load(b + 1, g)
                for t in range(4):
                    store(b, t)
                for g in range(NX, GROUPS_B):
                    load(b + 1, g)
                    if g % 2 and (g + 3) // 2 < TILES:
                        store(b, (g + 3) // 2)
            for t in range(TILES):
                store(B - 1, t)
            for t in range(TILES):
                sp.wait_ge(stored[t], 16 * B)

        @block.tensor
        def _(pe):
            pe.sem_inc(a_modes, 1)
            pe.wait_ge(const_in, 16 * n_const)
            pe.wait_ge(cw_ready, 1)
            pe.matmul(ps_main[:, 0, 0:P], cw2, dup[0:C, :], start=True, stop=True).then_inc(setup_mm, 1)
            pe.matmul(ps_main[:, 1, 0:3], dup[0:C, :], prm, start=True, stop=True).then_inc(setup_mm, 1)

            with pe.Fori(0, B) as b:
                with pe.Fori(0, A_TILES // NX) as q:
                    for s in range(NX):
                        pe.wait_ge(x_in[s], (b * (A_TILES // NX) + q + 1) * 16)
                        pe.wait_ge(a_copied, b * A_TILES + q * NX + s + 1)
                        ps = ps_slice[:, s % 2, 0:CH * 2 * KC].rearrange("p (c w k) -> p c w k", c=CH, w=2)
                        for c in range(CH):
                            for w in range(2):
                                for r in range(2):
                                    o = c * 512 + r * W + w * P
                                    mm = pe.matmul(ps[:, c, w, :], xa[s][:, o:o + P], dft_h[:, r, :],
                                                   start=(r == 0), stop=(r == 1))
                        mm.then_inc(a_sums, 1)
                pe.wait_ge(a_copied, (b + 1) * A_TILES + 2)
                pe.wait_ge(a_kept, b * 8 + 1)
                pe.wait_ge(setup_done, 5)
                for k in range(KH):
                    ps = ps_main[0:C, k // 8, k % 8 * 64:k % 8 * 64 + 64]
                    terms = [(w, t) for t in range(2 if k else 1) for w in range(2)]
                    for n, (w, t) in enumerate(terms):
                        mm = pe.matmul(ps, sums[:, w, k + t * MX, :], dft_w[:, w, t, :],
                                       start=(n == 0), stop=(n == len(terms) - 1))
                mm.then_inc(a_modes, 1)

            pe.wait_ge(a_kept, B * 8 + 1)
            for j in range(W_CHUNKS):
                pe.wait_ge(w_in[j % NW], 32 * (j // NW + 1))
                for xx in range(WX):
                    slot = WX * j + xx if j < W_CHUNKS // 2 else SLOTS - 1 - (WX * (j - W_CHUNKS // 2) + xx)
                    for half in range(2):
                        g = 8 * j + 2 * xx + half
                        if g >= 4:
                            pe.wait_ge(m_even if g % 2 == 0 else m_odd, (g - 4) // 2 + 1)
                        for y in range(8):
                            ky = 8 * half + y
                            mm = pe.matmul(ps_main[0:MODE, g % 4, y * C:(y + 1) * C],
                                           spec[:, slot, ky, :], wts[j % NW][:, :, xx * MY + ky],
                                           start=True, stop=True)
                        mm.then_inc(m_mixed, 1)

            def kh_inverse(b, sl, jj):
                n = JJ * (SL * b + sl) + jj
                if not at_start(n - 1):
                    pe.wait_ge(low, 2 * (n - 1))
                for i in range(8):
                    o = 2 * (8 * jj + i)
                    w = modes[:, o:o + 2].rearrange("p o d k -> p (o d k)")
                    mm = pe.matmul(ps_slice[:, jj % 2, i * 64:(i + 1) * 64], w,
                                   idft_h[0:C, sl * 64:(sl + 1) * 64], start=True, stop=True)
                mm.then_inc(kh_done, 1)

            def image(b, last):
                for t in range(TILES):
                    sl = t // SL_TILES
                    if sl + 1 < SL:
                        kh_inverse(b, sl + 1, t % SL_TILES)
                    if t % SL_TILES == 0:
                        pe.wait_ge(low, 2 * JJ * (SL * b + sl + 1))
                    for g in (2 * t, 2 * t + 1):
                        pe.wait_ge(xb_in[g % NX], 16 * (GROUPS_B // NX * b + g // NX + 1))
                        if not at_start(GROUPS_B * b + g - 1):
                            pe.wait_ge(gelu, GROUPS_B * b + g - 1)
                        for k in range(2):
                            o = k * BANK
                            bank = ps_main[:, 2 * (g % 2) + k, :]
                            pe.matmul(bank, mix[:], xb[g % NX][:, o:o + BANK], start=True, stop=True,
                                      skip_group_check=True)
                            for r in range(2):
                                row = (g * GRP + o) // W + r - sl * SL_ROWS
                                mm = pe.matmul(bank[:, r * W:(r + 1) * W], rows[sl % 2][:, row, :],
                                               idft_w[:], start=False, stop=True,
                                               skip_group_check=True)
                        mm.then_inc(pre, 1)
                pe.wait_ge(chain, 4 * b + 1)
                pe.matmul(ps_small[:, 0:1], group[:], mean_var[:, 0:1], start=True, stop=True
                          ).then_inc(gm_done, 1)
                pe.wait_ge(chain, 4 * b + 3)
                pe.matmul(ps_small[:, 1:2], group[:], spread, start=True, stop=True).then_inc(gm_done, 1)
                if not last:
                    pe.wait_ge(permuted, 2 * QC * (b + 2))
                    for jj in range(JJ):
                        kh_inverse(b + 1, 0, jj)

            pe.wait_ge(permuted, 2 * QC)
            for jj in range(JJ):
                kh_inverse(0, 0, jj)
            image(0, False)
            with pe.Fori(1, B - 1) as b:
                image(b, False)
            image(B - 1, True)

        @block.scalar
        def _(act):
            act.sem_inc(a_copied, 2)
            act.wait_ge(setup_mm, 2)
            nc.scalar.copy(params[:], ps_main[:, 1, 0:3]).then_inc(setup_done, 1)
            nc.scalar.copy(idft_w[:], idft_w_raw).then_inc(setup_done, 1)

            with act.Fori(0, B) as b:
                act.wait_ge(a_modes, b + 1)
                with act.Fori(0, A_TILES // NX) as q:
                    for s in range(NX):
                        act.wait_ge(a_sums, b * A_TILES + q * NX + s + 1)
                        ps = ps_slice[:, s % 2, 0:CH * 2 * KC].rearrange("p (c w k) -> p w k c", c=CH, w=2)
                        nc.scalar.copy(sums[:, :, :, bass.ds((q * NX + s) * CH, CH)], ps
                                       ).then_inc(a_copied, 1)

            def keep(g, engine_copy, done):
                j, xx, half = g // 8, g // 2 % WX, g % 2
                place = xx if j < W_CHUNKS // 2 else WX - 1 - xx
                dst = mixed[j % 2][:, place, :].rearrange("p (o k) -> p o k", k=MY)[:, :, 8 * half:8 * half + 8]
                engine_copy(dst, ps_main[0:MODE, g % 4, :].rearrange("p (k o) -> p o k", o=C)
                            ).then_inc(done, 1)

            for g in range(0, 8 * W_CHUNKS, 2):
                act.wait_ge(m_mixed, g + 1)
                if g % 8 == 0 and g >= 16:
                    act.wait_ge(m_out[g // 8 % 2], 16 * (g // 16))
                keep(g, nc.scalar.copy, m_even)

            def high_parts(b, sl, jj):
                n = JJ * (SL * b + sl) + jj
                act.wait_ge(kh_done, n + 1)
                if jj == 0 and not at_start(SL * b + sl - 1):
                    act.wait_ge(pre, 8 * (SL * b + sl - 1))
                for q in range(2):
                    dst = rows[sl % 2][0:C].rearrange("p r (j q s) -> p j q r s", q=2, s=2)
                    src = ps_slice[q * C:(q + 1) * C, jj % 2, :].rearrange("p (j r s) -> p j r s", j=8, s=2)
                    nc.scalar.copy(dst[:, 8 * jj:8 * jj + 8, q], src).then_inc(high, 1)

            def image(b, last):
                for t in range(TILES):
                    if t // SL_TILES + 1 < SL:
                        high_parts(b, t // SL_TILES + 1, t % SL_TILES)
                    if not at_start(b):
                        act.wait_ge(stored[t], 16 * b)
                    for g in (2 * t, 2 * t + 1):
                        act.wait_ge(pre, GROUPS_B * b + g + 1)
                        o = g % 2 * GRP
                        nc.scalar.activation(home[:, t, o:o + GRP],
                                             ps_main[:, 2 * (g % 2):2 * (g % 2) + 2, :].rearrange("p a n -> p (a n)"),
                                             ACT.Gelu, bias=params[:, 0:1]).then_inc(gelu, 1)
                if not last:
                    for jj in range(JJ):
                        high_parts(b + 1, 0, jj)

            act.wait_ge(setup_done, 5)
            for jj in range(JJ):
                high_parts(0, 0, jj)
            image(0, False)
            with act.Fori(1, B - 1) as b:
                image(b, False)
            image(B - 1, True)

        @block.vector
        def _(dve):
            dve.sem_inc(a_kept, 1)
            dve.wait_ge(const_in, 16 * n_const)
            nc.vector.tensor_copy(cw2.rearrange("p (c s) -> p c s", s=2),
                                  cw.unsqueeze(2).broadcast_to([C, C, 2])).then_inc(cw_ready, 1)
            dve.wait_ge(setup_mm, 2)
            nc.vector.tensor_tensor(prod, ps_main[:, 0, 0:P], same_half, ALU.mult).then_inc(mask_done, 1)
            dve.wait_ge(mask_done, 1)
            nc.vector.tensor_tensor(mix[:], prod, ident, ALU.add).then_inc(setup_done, 3)

            with dve.Fori(0, B) as b:
                dve.wait_ge(a_modes, b + 2)
                ps = ps_main[0:C, 0:3, :].rearrange("p a n -> p (a n)")[:, 0:KH * 64]
                ps = ps.rearrange("p (k g r y) -> p k g r y", g=2, r=2, y=MY)
                for sign in range(2):
                    src = ps[:, sign:sign + MX, sign]
                    for half in range(2):
                        dst = spec[half * C:(half + 1) * C, sign * MX:(sign + 1) * MX]
                        dst = dst.rearrange("p k y (r b) -> p k r y b", r=2)
                        for r in range(2):
                            d = dst[:, :, r, :, bass.ds(b, 1)].rearrange("p k y a -> p k (y a)")
                            if half == 0:
                                nc.vector.tensor_copy(d, src[:, :, r]).then_inc(a_kept, 1)
                            elif r == 0:
                                nc.vector.tensor_scalar(d, src[:, :, 1], -1.0, None, ALU.mult
                                                        ).then_inc(a_kept, 1)
                            else:
                                nc.vector.tensor_copy(d, src[:, :, 0]).then_inc(a_kept, 1)

            for g in range(1, 8 * W_CHUNKS, 2):
                j, xx = g // 8, g // 2 % WX
                dve.wait_ge(m_mixed, g + 1)
                if g % 8 == 1 and g >= 16:
                    dve.wait_ge(m_out[j % 2], 16 * (j // 2))
                place = xx if j < W_CHUNKS // 2 else WX - 1 - xx
                dst = mixed[j % 2][:, place, :].rearrange("p (o k) -> p o k", k=MY)[:, :, 8:16]
                nc.vector.tensor_copy(dst, ps_main[0:MODE, g % 4, :].rearrange("p (k o) -> p o k", o=C)
                                      ).then_inc(m_odd, 1)

            def low_parts(b, sl, jj):
                n = JJ * (SL * b + sl) + jj
                for q in range(2):
                    dve.wait_ge(high, 2 * n + q + 1)
                    sel = [rows[sl % 2][i * C:(i + 1) * C].rearrange("p r (j q s) -> p j q r s", q=2, s=2)
                           [:, 8 * jj:8 * jj + 8, q] for i in range(2)]
                    src = ps_slice[q * C:(q + 1) * C, jj % 2, :].rearrange("p (j r s) -> p j r s", j=8, s=2)
                    nc.vector.tensor_tensor(sel[1], src, sel[0].bitcast(F32), ALU.subtract).then_inc(low, 1)

            def norm(b, t):
                nc.vector.tensor_scalar(home[:, t, :], home[:, t, :], scale, shift, ALU.mult, ALU.add
                                        ).then_inc(normed, 1)

            def image(b, last):
                for t in range(TILES):
                    if t // SL_TILES + 1 < SL:
                        low_parts(b, t // SL_TILES + 1, t % SL_TILES)
                    for g in (2 * t, 2 * t + 1):
                        dve.wait_ge(gelu, GROUPS_B * b + g + 1)
                        for k in range(2):
                            o = g % 2 * GRP + k * BANK
                            nc.vector.bn_stats(stats[:, 2 * g + k, :], home[:, t, o:o + BANK]).then_inc(bn, 1)
                dve.wait_ge(bn, 4 * TILES * (b + 1))
                dve.sem_inc(bn_all, 1)
                nc.vector.bn_aggr(mean_var, stats[:].rearrange("p a n -> p (a n)")).then_inc(chain, 1)
                dve.wait_ge(gm_done, 2 * b + 1)
                nc.vector.tensor_tensor(dev, mean_var[:, 0:1], ps_small[:, 0:1], ALU.subtract).then_inc(chain, 1)
                dve.wait_ge(chain, 4 * b + 2)
                nc.vector.scalar_tensor_tensor(out=spread, in0=dev, scalar=dev, in1=mean_var[:, 1:2],
                                               op0=ALU.mult, op1=ALU.add).then_inc(chain, 1)
                dve.wait_ge(gm_done, 2 * b + 2)
                nc.vector.tensor_scalar(var_eps, ps_small[:, 1:2], EPS, None, ALU.add).then_inc(chain, 1)
                dve.wait_ge(rstd_done, b + 1)
                nc.vector.tensor_tensor(scale, rstd, params[:, 1:2], ALU.mult).then_inc(scaled, 1)
                dve.wait_ge(scaled, 3 * b + 1)
                nc.vector.tensor_tensor(shift0, scale, ps_small[:, 0:1], ALU.mult).then_inc(scaled, 1)
                dve.wait_ge(scaled, 3 * b + 2)
                nc.vector.tensor_tensor(shift, params[:, 2:3], shift0, ALU.subtract).then_inc(scaled, 1)
                dve.wait_ge(scaled, 3 * b + 3)
                for t in range(TILES):
                    norm(b, t)
                    if not last and t < JJ:
                        low_parts(b + 1, 0, t)

            for jj in range(JJ):
                low_parts(0, 0, jj)
            image(0, False)
            with dve.Fori(1, B - 1) as b:
                image(b, False)
            image(B - 1, True)

        @block.gpsimd
        def _(pool):
            for i in range(2):
                pool.wait_ge(m_out[i], 16 * (W_CHUNKS // 2))
            src = scratch.rearrange("(r b) k n -> r b k n", r=2)

            def quarter(b, qt):
                if not at_start(QC * b + qt):
                    pool.wait_ge(permuted, 2 * (QC * b + qt))
                for first in range(2):
                    for r in range(2):
                        part = src[(r + first) % 2, bass.ds(b, 1), :, qt * QO * MY:(qt + 1) * QO * MY]
                        pool.dma_start(raw[r * SLOTS:(r + 1) * SLOTS, first, :],
                                       part.rearrange("a k n -> (a k) n")).then_inc(raw_in, 16)
                pool.wait_ge(raw_in, 64 * (QC * b + qt + 1))
                if qt == 0 and not at_start(b):
                    pool.wait_ge(kh_done, JJ * SL * b)
                pool.sem_inc(quarter_in, 1)
                dst = modes[:, qt * QO:(qt + 1) * QO].rearrange("p o d (r k) -> p r o d k", r=2)
                one, two = (raw[:, i, :].rearrange("p (o k) -> p o k", k=MY).unsqueeze(2)
                            .broadcast_to([C, QO, 2, MY]) for i in range(2))
                nc.gpsimd.tensor_copy(dst[:, 0], one).then_inc(permuted, 1)
                nc.gpsimd.tensor_scalar(dst[:, 1], two, signs[0:C, 0:1], None, ALU.mult).then_inc(permuted, 1)

            def root(b):
                pool.wait_ge(chain, 4 * b + 4)
                nc.gpsimd.tensor_tensor(rstd, var_eps, signs[:, 1:2], ALU.pow).then_inc(rstd_done, 1)

            for qt in range(QC):
                quarter(0, qt)
            with pool.Fori(0, B - 1) as b:
                for qt in range(QC):
                    quarter(b + 1, qt)
                root(b)
            root(B - 1)


_INS = ["x", "L0_conv_w1_re", "L0_conv_w1_im", "L0_conv_w2_re", "L0_conv_w2_im", "L0_conv_conv_w",
        "L0_conv_conv_b", "L0_conv_gn_w", "L0_conv_gn_b"]


def kernel(**inputs):
    import concourse.bacc as _bacc
    from concourse.bass_utils import run_bass_kernel_spmd as _run

    nc = _bacc.Bacc("TRN2", target_bir_lowering=False, num_devices=1)
    arrays, args = {}, []
    for name in _INS:
        a = np.ascontiguousarray(inputs[name])
        arrays[f"in_{name}"] = a
        args.append(nc.dram_tensor(f"in_{name}", a.shape, F32, kind="ExternalInput").ap())
    arrays["in_constants"] = constants()
    args.append(nc.dram_tensor("in_constants", arrays["in_constants"].shape, F32, kind="ExternalInput").ap())
    args.append(nc.dram_tensor("out", (B, C, H, W), F32, kind="ExternalOutput").ap())
    fno_layer(nc, *args)
    r = _run(nc, [arrays], core_ids=[0])
    return r.results[0]["out"]
```

```python
from contextlib import ExitStack

import numpy as np

import concourse.bass as bass
from concourse import mybir

F32 = mybir.dt.float32
F32R = mybir.dt.float32r
ALU = mybir.AluOpType
ACT = mybir.ActivationFunctionType

B, C, H, W = 16, 64, 256, 256
MX, MY = 16, 16
GROUPS = 32
EPS = 1e-5
P = 128
HH = H // 2
KH = MX + 1
KC = KH + MX
SLOTS = 2 * MX
RI = 2
MODE = 2 * B

CH = 4
NX = 4
NF = 64
TILE = 2048
A_TILES = C // CH

WX = 4
NW = 3
W_CHUNKS = 2 * MX // WX

TILES = HH * W // TILE
GRP = 1024
BANK = 512
GROUPS_B = HH * W // GRP
SL = 4
SL_ROWS = HH // SL
SL_TILES = TILES // SL
QUAD = 4
JJ = 2
LEAD = 3
NXB = NX * TILE // GRP
HC = C // JJ

CONST_COLS = {
    "dft_h": 2 * NF, "dft_w": 2 * 2 * 64, "idft_h": 256, "idft_w": 256, "group": P,
    "dup": P, "same_half": P, "ident": P, "sign": 1, "neg_half": 1,
}


def top12(a):
    u = np.asarray(a, np.float32).view(np.uint32).astype(np.uint64)
    u = (u + 0x7FF + ((u >> 12) & 1)) & 0xFFFFF000
    return u.astype(np.uint32).view(np.float32)


def at_start(n):
    return isinstance(n, int) and n <= 0


def constants():
    c = {}
    p = np.arange(P)
    k = np.arange(KH)
    dft_h = np.zeros((P, 2, NF))
    for r in range(2):
        angle = 2 * np.pi * ((2 * p + r)[:, None] * k[None, :] % H) / H
        dft_h[:, r, :KH] = np.cos(angle)
        dft_h[:, r, KH:KC] = np.sin(angle)[:, 1:]
    c["dft_h"] = dft_h
    dft_w = np.zeros((P, 2, 2, 2, RI, MY))
    for chunk in range(2):
        angle = 2 * np.pi * ((P * chunk + p)[:, None] * np.arange(MY)[None, :] % W) / W
        cos, sin = np.cos(angle), np.sin(angle)
        for sign, s in ((0, 1), (1, -1)):
            dft_w[:, chunk, 0, sign, 0] = cos
            dft_w[:, chunk, 0, sign, 1] = -sin
            dft_w[:, chunk, 1, sign, 0] = -s * sin
            dft_w[:, chunk, 1, sign, 1] = -s * cos
    c["dft_w"] = dft_w
    kh = np.concatenate([np.arange(MX), -1 - np.arange(MX)])
    h = (np.arange(HH)[:, None] + HH * np.arange(2)[None, :]).ravel()
    angle = 2 * np.pi * (kh[:, None] * h[None, :] % H) / H
    c["idft_h"] = np.concatenate([np.cos(angle), -np.sin(angle)])
    angle = 2 * np.pi * (np.arange(MY)[:, None] * np.arange(W)[None, :] % W) / W
    twice = np.where(np.arange(MY) > 0, 2.0, 1.0)[:, None] / (H * W)
    e = np.concatenate([twice * np.cos(angle), -twice * np.sin(angle)]).astype(np.float32)
    high = top12(e)
    low = top12(e - high)
    c["idft_w"] = np.concatenate([high, low, high, low])
    span = 2 * C // GROUPS
    c["group"] = (p[:, None] // span == p[None, :] // span) / span
    c["dup"] = np.zeros((P, P))
    c["dup"][:C] = np.arange(C)[:, None] == p[None, :] // 2
    c["same_half"] = p[:, None] % 2 == p[None, :] % 2
    c["ident"] = np.eye(P)
    c["sign"] = np.where(p % (2 * SLOTS) < SLOTS, 1.0, -1.0)
    c["neg_half"] = np.full(P, -0.5)
    return np.concatenate([np.asarray(c[n], np.float32).reshape(P, -1) if c[n].shape[0] == P else
                           np.pad(np.asarray(c[n], np.float32), ((0, P - c[n].shape[0]), (0, 0)))
                           for n in CONST_COLS], axis=1)


def fno_layer(nc, x, w1_re, w1_im, w2_re, w2_im, conv_w, conv_b, gn_w, gn_b, const, out):
    ctx = ExitStack()
    with ctx:
        def sb(name, shape, dt=F32, stack=ctx):
            return stack.enter_context(nc.sbuf_tensor(name, shape, dt))

        def psum(name, shape):
            return ctx.enter_context(nc.psum_tensor(name, shape, F32))

        def sem(name):
            return ctx.enter_context(nc.semaphore(name))

        xs = [sb(f"x_tile{i}", [P, TILE]) for i in range(NX)]
        xb = [xs[i // 2][:, i % 2 * GRP:(i % 2 + 1) * GRP] for i in range(NXB)]
        idft_h = sb("idft_h", [P, 256])
        idft_w = sb("idft_w", [P, 256], F32R)
        group = sb("group", [P, P])
        mix = sb("mix", [P, P])
        params = sb("params", [P, 3])
        signs = sb("signs", [P, 2])

        early = ExitStack()
        dft_h = sb("dft_h", [P, 2, NF], stack=early)
        dft_w = sb("dft_w", [P, 2, 2, 64], stack=early)
        sums = sb("sums", [P, 2, KC, C], stack=early)
        spec = sb("spec", [P, SLOTS, MY, MODE], stack=early)
        wts = [sb(f"weights{i}", [P, C, WX * MY], stack=early) for i in range(NW)]
        mixed = [sb(f"mixed{i}", [MODE, WX, C * MY], stack=early) for i in range(2)]
        once = wts[NW - 1][:].rearrange("p a b -> p (a b)")
        dup = once[:, 0:P]
        same_half = once[:, P:2 * P]
        ident = once[:, 2 * P:3 * P]
        idft_w_raw = once[:, 3 * P:5 * P]
        cw = once[0:C, 5 * P:5 * P + C]
        cw2 = once[0:C, 6 * P:7 * P]
        prm = once[0:C, 7 * P:7 * P + 3]
        prod = once[:, 8 * P:9 * P]
        early.close()

        home = sb("home", [P, TILES, TILE])
        rows = [sb(f"row_modes{i}", [P, SL_ROWS, P], F32R) for i in range(2)]
        both = sb("modes", [P, C * RI * MY])
        modes = both[0:C].rearrange("p (o k) -> p o k", o=C)
        raw = both[C:P].rearrange("p (r o k) -> p r o k", r=RI, o=C)
        stats = sb("stats", [P, TILES * 4, 6])
        small = sb("small", [P, 12])
        mean_var, dev, spread = small[:, 0:2], small[:, 2:3], small[:, 3:4]
        var_eps, rstd, scale, shift0, shift = (small[:, i:i + 1] for i in range(4, 9))
        gmean = small[:, 9:10]

        scratch = nc.dram_tensor("mixed_modes", [RI * B, SLOTS, C * MY], F32).ap()

        ps_main = psum("ps_main", [P, 4, BANK])
        ps_slice = psum("ps_slice", [P, 2, BANK])
        ps_small = psum("ps_small", [P, BANK])

        const_in = sem("const_in")
        cw_ready = sem("cw_ready")
        setup_mm = sem("setup_mm")
        mask_done = sem("mask_done")
        setup_done = sem("setup_done")
        x_in = [sem(f"x_in{i}") for i in range(NX)]
        xb_in = [sem(f"xb_in{i}") for i in range(NXB)]
        w_in = [sem(f"w_in{i}") for i in range(NW)]
        a_sums = sem("a_sums")
        a_copied = sem("a_copied")
        a_modes = sem("a_modes")
        a_kept = sem("a_kept")
        m_mixed = sem("m_mixed")
        m_even = sem("m_even")
        m_odd = sem("m_odd")
        m_out = [sem(f"m_out{i}") for i in range(2)]
        raw_in = sem("raw_in")
        permuted = sem("permuted")
        kh_done = sem("kh_done")
        high = sem("high")
        low = sem("low")
        low2 = sem("low2")
        pre = sem("pre")
        gelu = sem("gelu")
        bn = sem("bn")
        bn_all = sem("bn_all")
        modes_free = sem("modes_free")
        chain = sem("chain")
        scaled = sem("scaled")
        gm_done = sem("gm_done")
        rstd_done = sem("rstd_done")
        normed = sem("normed")
        stored = [sem(f"stored{i}") for i in range(TILES)]

        x_a = x.rearrange("b c (p r) w -> p (b c) (r w)", r=2)
        x_b = x.rearrange("b c h w -> b (c h w)").rearrange("b (p n) -> p b n", p=P)
        out_b = out.rearrange("b c h w -> b (c h w)").rearrange("b (p n) -> p b n", p=P)
        col = {}
        at = 0
        for n, k in CONST_COLS.items():
            col[n] = const[:, at:at + k]
            at += k

        n_const = 13
        block = ctx.enter_context(nc.Block())

        @block.sync
        def _(sp):
            sp.dma_start(dft_h[:].rearrange("p a b -> p (a b)"), col["dft_h"]).then_inc(const_in, 16)
            sp.dma_start(dft_w[:].rearrange("p a b c -> p (a b c)"), col["dft_w"]).then_inc(const_in, 16)
            for s in range(NX):
                sp.dma_start(xs[s][:].rearrange("p (c n) -> p c n", c=CH),
                             x_a[:, s * CH:(s + 1) * CH, :]).then_inc(x_in[s], 16)
            sp.dma_start(idft_h[:], col["idft_h"]).then_inc(const_in, 16)
            sp.dma_start(idft_w_raw, col["idft_w"]).then_inc(const_in, 16)
            sp.dma_start(group[:], col["group"]).then_inc(const_in, 16)
            sp.dma_start(dup, col["dup"]).then_inc(const_in, 16)
            sp.dma_start(same_half, col["same_half"]).then_inc(const_in, 16)
            sp.dma_start(ident, col["ident"]).then_inc(const_in, 16)
            sp.dma_start(signs[:], const[:, at - 2:at]).then_inc(const_in, 16)
            sp.dma_start(cw, conv_w).then_inc(const_in, 16)
            for i, v in enumerate((conv_b, gn_w, gn_b)):
                sp.dma_start(prm[:, i:i + 1], v.rearrange("(c a) -> c a", a=1)).then_inc(const_in, 16)

            def weights(j):
                xx = WX * (j % (W_CHUNKS // 2))
                re, im = (w1_re, w1_im) if j < W_CHUNKS // 2 else (w2_re, w2_im)
                for half, w in ((0, re), (1, im)):
                    sp.dma_start(wts[j % NW][half * C:(half + 1) * C],
                                 w[:, :, xx:xx + WX, :].rearrange("i o x y -> i o (x y)")
                                 ).then_inc(w_in[j % NW], 16)

            sp.wait_ge(setup_done, 5)
            for j in range(NW):
                weights(j)
            with sp.Fori(1, B * A_TILES // NX) as u:
                for s in range(NX):
                    sp.wait_ge(a_sums, (u - 1) * NX + s + 1)
                    sp.dma_start(xs[s][:].rearrange("p (c n) -> p c n", c=CH),
                                 x_a[:, bass.ds((u * NX + s) * CH, CH), :]).then_inc(x_in[s], 16)

            def fetch(b, g):
                sp.dma_start(xb[g % NXB], x_b[:, bass.ds(b, 1), g * GRP:(g + 1) * GRP]
                             .rearrange("p a n -> p (a n)")).then_inc(xb_in[g % NXB], 16)

            for g in range(NXB):
                sp.wait_ge(a_sums, B * A_TILES - NX + g // 2 + 1)
                fetch(0, g)
            for j in range(W_CHUNKS):
                if j + NW < W_CHUNKS:
                    sp.wait_ge(m_mixed, (j + 1) * 8)
                    weights(j + NW)
                sp.wait_ge(m_even, (j + 1) * 4)
                sp.wait_ge(m_odd, (j + 1) * 4)
                first = WX * j if j < W_CHUNKS // 2 else SLOTS - WX * (j - W_CHUNKS // 2 + 1)
                sp.dma_start(scratch[:, first:first + WX, :], mixed[j % 2][:]).then_inc(m_out[j % 2], 16)

            def load(b, g):
                sp.wait_ge(pre, GROUPS_B * b + g - NXB + 1)
                fetch(b, g)

            def store(b, t):
                sp.wait_ge(normed, TILES * b + t + 1)
                sp.dma_start(out_b[:, bass.ds(b, 1), t * TILE:(t + 1) * TILE]
                             .rearrange("p a n -> p (a n)"), home[:, t, :]).then_inc(stored[t], 16)

            for g in range(NXB, GROUPS_B):
                load(0, g)
            with sp.Fori(0, B - 1) as b:
                for g in range(NXB):
                    load(b + 1, g)
                for t in range(LEAD):
                    store(b, t)
                for g in range(NXB, GROUPS_B):
                    load(b + 1, g)
                    if g % 2:
                        store(b, LEAD + (g - NXB) // 2)
                for t in range(LEAD + (GROUPS_B - NXB) // 2, TILES):
                    store(b, t)
            for t in range(TILES):
                store(B - 1, t)
            for t in range(TILES):
                sp.wait_ge(stored[t], 16 * B)

        @block.tensor
        def _(pe):
            pe.sem_inc(a_modes, 1)
            pe.wait_ge(const_in, 16 * n_const)
            pe.wait_ge(cw_ready, 1)
            pe.matmul(ps_main[:, 0, 0:P], cw2, dup[0:C, :], start=True, stop=True).then_inc(setup_mm, 1)
            pe.matmul(ps_main[:, 1, 0:3], dup[0:C, :], prm, start=True, stop=True).then_inc(setup_mm, 1)

            with pe.Fori(0, B) as b:
                with pe.Fori(0, A_TILES // NX) as q:
                    for s in range(NX):
                        pe.wait_ge(x_in[s], (b * (A_TILES // NX) + q + 1) * 16)
                        pe.wait_ge(a_copied, b * A_TILES + q * NX + s + 1)
                        ps = ps_slice[:, s % 2, 0:CH * 2 * NF].rearrange("p (c w k) -> p c w k", c=CH, w=2)
                        for c in range(CH):
                            for w in range(2):
                                for r in range(2):
                                    o = c * 512 + r * W + w * P
                                    mm = pe.matmul(ps[:, c, w, :], xs[s][:, o:o + P], dft_h[:, r, :],
                                                   start=(r == 0), stop=(r == 1))
                        mm.then_inc(a_sums, 1)
                pe.wait_ge(a_copied, (b + 1) * A_TILES + 2)
                pe.wait_ge(a_kept, b * 8 + 1)
                pe.wait_ge(setup_done, 5)
                for k in range(KH):
                    ps = ps_main[0:C, k // 8, k % 8 * 64:k % 8 * 64 + 64]
                    terms = [(w, t) for t in range(2 if k else 1) for w in range(2)]
                    for n, (w, t) in enumerate(terms):
                        mm = pe.matmul(ps, sums[:, w, k + t * MX, :], dft_w[:, w, t, :],
                                       start=(n == 0), stop=(n == len(terms) - 1))
                mm.then_inc(a_modes, 1)

            pe.wait_ge(a_kept, B * 8 + 1)
            for j in range(W_CHUNKS):
                pe.wait_ge(w_in[j % NW], 32 * (j // NW + 1))
                for xx in range(WX):
                    slot = WX * j + xx if j < W_CHUNKS // 2 else SLOTS - 1 - (WX * (j - W_CHUNKS // 2) + xx)
                    for half in range(2):
                        g = 8 * j + 2 * xx + half
                        if g >= 4:
                            pe.wait_ge(m_even if g % 2 == 0 else m_odd, (g - 4) // 2 + 1)
                        for y in range(8):
                            ky = 8 * half + y
                            mm = pe.matmul(ps_main[0:MODE, g % 4, y * C:(y + 1) * C],
                                           spec[:, slot, ky, :], wts[j % NW][:, :, xx * MY + ky],
                                           start=True, stop=True)
                        mm.then_inc(m_mixed, 1)

            def kh_inverse(b, sl, jj):
                n = JJ * (SL * b + sl) + jj
                if not at_start(n - 1):
                    pe.wait_ge(low, QUAD * (n - 1))
                if sl == 0:
                    pe.wait_ge(permuted, 2 * (JJ * b + jj + 1))
                for i in range(8):
                    o = QUAD * (8 * jj + i)
                    w = modes[:, o:o + QUAD, :].rearrange("p o k -> p (o k)")
                    mm = pe.matmul(ps_slice[:, jj, i * 64:(i + 1) * 64], w,
                                   idft_h[0:C, sl * 64:(sl + 1) * 64], start=True, stop=True)
                mm.then_inc(kh_done, 1)

            def image(b, last):
                for t in range(TILES):
                    sl = t // SL_TILES
                    if t % 2 == 0 and not (last and sl == SL - 1):
                        kh_inverse(b + (sl + 1) // SL, (sl + 1) % SL, t % SL_TILES // 2)
                    if t % SL_TILES == 0:
                        pe.wait_ge(low2, JJ * (SL * b + sl + 1))
                    for g in (2 * t, 2 * t + 1):
                        pe.wait_ge(xb_in[g % NXB], 16 * (GROUPS_B // NXB * b + g // NXB + 1))
                        if not at_start(GROUPS_B * b + g - 1):
                            pe.wait_ge(gelu, GROUPS_B * b + g - 1)
                        for k in range(2):
                            o = k * BANK
                            bank = ps_main[:, 2 * (g % 2) + k, :]
                            pe.matmul(bank, mix[:], xb[g % NXB][:, o:o + BANK], start=True, stop=True,
                                      skip_group_check=True)
                            for r in range(2):
                                row = (g * GRP + o) // W + r - sl * SL_ROWS
                                mm = pe.matmul(bank[:, r * W:(r + 1) * W], rows[sl % 2][:, row, :],
                                               idft_w[:], start=False, stop=True,
                                               skip_group_check=True)
                        mm.then_inc(pre, 1)
                pe.wait_ge(chain, 4 * b + 1)
                pe.matmul(ps_small[:, 0:1], group[:], mean_var[:, 0:1], start=True, stop=True
                          ).then_inc(gm_done, 1)
                pe.wait_ge(chain, 4 * b + 3)
                pe.matmul(ps_small[:, 1:2], group[:], spread, start=True, stop=True).then_inc(gm_done, 1)

            for jj in range(JJ):
                kh_inverse(0, 0, jj)
            image(0, False)
            with pe.Fori(1, B - 1) as b:
                image(b, False)
            image(B - 1, True)

        @block.scalar
        def _(act):
            act.sem_inc(a_copied, 2)
            act.wait_ge(setup_mm, 2)
            nc.scalar.copy(params[:], ps_main[:, 1, 0:3]).then_inc(setup_done, 1)
            nc.scalar.copy(idft_w[:], idft_w_raw).then_inc(setup_done, 1)

            with act.Fori(0, B) as b:
                act.wait_ge(a_modes, b + 1)
                with act.Fori(0, A_TILES // NX) as q:
                    for s in range(NX):
                        act.wait_ge(a_sums, b * A_TILES + q * NX + s + 1)
                        ps = ps_slice[:, s % 2, 0:CH * 2 * NF].rearrange("p (c w k) -> p w k c", c=CH, w=2)[:, :, 0:KC]
                        nc.scalar.copy(sums[:, :, :, bass.ds((q * NX + s) * CH, CH)], ps
                                       ).then_inc(a_copied, 1)

            def keep(g, engine_copy, done):
                j, xx, half = g // 8, g // 2 % WX, g % 2
                place = xx if j < W_CHUNKS // 2 else WX - 1 - xx
                dst = mixed[j % 2][:, place, :].rearrange("p (o k) -> p o k", k=MY)[:, :, 8 * half:8 * half + 8]
                engine_copy(dst, ps_main[0:MODE, g % 4, :].rearrange("p (k o) -> p o k", o=C)
                            ).then_inc(done, 1)

            for g in range(0, 8 * W_CHUNKS, 2):
                act.wait_ge(m_mixed, g + 1)
                if g % 8 == 0 and g >= 16:
                    act.wait_ge(m_out[g // 8 % 2], 16 * (g // 16))
                keep(g, nc.scalar.copy, m_even)

            def high_parts(b, sl, jj):
                n = JJ * (SL * b + sl) + jj
                act.wait_ge(kh_done, n + 1)
                if jj == 0 and not at_start(SL * b + sl - 1):
                    act.wait_ge(pre, 8 * (SL * b + sl - 1))
                for q in range(QUAD):
                    for copy in range(2):
                        dst = rows[sl % 2][32 * copy:32 * copy + 32].rearrange(
                            "p r (j q s) -> p j q r s", q=QUAD, s=2)[:, 8 * jj:8 * jj + 8, q]
                        src = ps_slice[32 * q:32 * q + 32, jj, :].rearrange("p (j r s) -> p j r s", j=8, s=2)
                        part = nc.scalar.copy(dst, src)
                    part.then_inc(high, 1)

            def low_again(b, sl, jj):
                n = JJ * (SL * b + sl) + jj
                act.wait_ge(low, QUAD * (n + 1))
                part = [rows[sl % 2][32 * i:32 * i + 32, :, 64 * jj:64 * jj + 64] for i in (2, 3)]
                nc.scalar.copy(part[1], part[0].bitcast(F32)).then_inc(low2, 1)

            def image(b, last):
                for t in range(TILES):
                    nxt = t // SL_TILES + 1
                    if not (last and nxt == SL):
                        step = high_parts if t % 2 == 0 else low_again
                        step(b + nxt // SL, nxt % SL, t % SL_TILES // 2)
                    if not at_start(b):
                        act.wait_ge(stored[t], 16 * b)
                    for g in (2 * t, 2 * t + 1):
                        act.wait_ge(pre, GROUPS_B * b + g + 1)
                        o = g % 2 * GRP
                        nc.scalar.activation(home[:, t, o:o + GRP],
                                             ps_main[:, 2 * (g % 2):2 * (g % 2) + 2, :].rearrange("p a n -> p (a n)"),
                                             ACT.Gelu, bias=params[:, 0:1]).then_inc(gelu, 1)

            act.wait_ge(setup_done, 5)
            for step in (high_parts, low_again):
                for jj in range(JJ):
                    step(0, 0, jj)
            image(0, False)
            with act.Fori(1, B - 1) as b:
                image(b, False)
            image(B - 1, True)

        @block.vector
        def _(dve):
            dve.sem_inc(a_kept, 1)
            dve.wait_ge(const_in, 16 * n_const)
            nc.vector.tensor_copy(cw2.rearrange("p (c s) -> p c s", s=2),
                                  cw.unsqueeze(2).broadcast_to([C, C, 2])).then_inc(cw_ready, 1)
            dve.wait_ge(setup_mm, 2)
            nc.vector.tensor_tensor(prod, ps_main[:, 0, 0:P], same_half, ALU.mult).then_inc(mask_done, 1)
            dve.wait_ge(mask_done, 1)
            nc.vector.tensor_tensor(mix[:], prod, ident, ALU.add).then_inc(setup_done, 3)

            with dve.Fori(0, B) as b:
                dve.wait_ge(a_modes, b + 2)
                ps = ps_main[0:C, 0:3, :].rearrange("p a n -> p (a n)")[:, 0:KH * 64]
                ps = ps.rearrange("p (k g r y) -> p k g r y", g=2, r=2, y=MY)
                for sign in range(2):
                    src = ps[:, sign:sign + MX, sign]
                    for half in range(2):
                        dst = spec[half * C:(half + 1) * C, sign * MX:(sign + 1) * MX]
                        dst = dst.rearrange("p k y (r b) -> p k r y b", r=2)
                        for r in range(2):
                            d = dst[:, :, r, :, bass.ds(b, 1)].rearrange("p k y a -> p k (y a)")
                            if half == 0:
                                nc.vector.tensor_copy(d, src[:, :, r]).then_inc(a_kept, 1)
                            elif r == 0:
                                nc.vector.tensor_scalar(d, src[:, :, 1], -1.0, None, ALU.mult
                                                        ).then_inc(a_kept, 1)
                            else:
                                nc.vector.tensor_copy(d, src[:, :, 0]).then_inc(a_kept, 1)

            for g in range(1, 8 * W_CHUNKS, 2):
                j, xx = g // 8, g // 2 % WX
                dve.wait_ge(m_mixed, g + 1)
                if g % 8 == 1 and g >= 16:
                    dve.wait_ge(m_out[j % 2], 16 * (j // 2))
                place = xx if j < W_CHUNKS // 2 else WX - 1 - xx
                dst = mixed[j % 2][:, place, :].rearrange("p (o k) -> p o k", k=MY)[:, :, 8:16]
                nc.vector.tensor_copy(dst, ps_main[0:MODE, g % 4, :].rearrange("p (k o) -> p o k", o=C)
                                      ).then_inc(m_odd, 1)

            def low_parts(b, sl, jj):
                n = JJ * (SL * b + sl) + jj
                for q in range(QUAD):
                    dve.wait_ge(high, QUAD * n + q + 1)
                    part = [rows[sl % 2][32 * i:32 * i + 32].rearrange("p r (j q s) -> p j q r s", q=QUAD, s=2)
                            [:, 8 * jj:8 * jj + 8, q] for i in (0, 2)]
                    src = ps_slice[32 * q:32 * q + 32, jj, :].rearrange("p (j r s) -> p j r s", j=8, s=2)
                    nc.vector.tensor_tensor(part[1], src, part[0].bitcast(F32), ALU.subtract).then_inc(low, 1)

            def norm(t):
                nc.vector.tensor_scalar(home[:, t, :], home[:, t, :], scale, shift, ALU.mult, ALU.add
                                        ).then_inc(normed, 1)

            def image(b, first, last):
                if not first:
                    for t in range(LEAD):
                        norm(t)
                for t in range(TILES):
                    if not first:
                        for o in range(LEAD + 2 * t, min(LEAD + 2 * t + 2, TILES)):
                            norm(o)
                    nxt = t // SL_TILES + 1
                    if t % 2 == 0 and not (last and nxt == SL):
                        low_parts(b + nxt // SL, nxt % SL, t % SL_TILES // 2)
                    for g in (2 * t, 2 * t + 1):
                        dve.wait_ge(gelu, GROUPS_B * b + g + 1)
                        for k in range(2):
                            o = g % 2 * GRP + k * BANK
                            nc.vector.bn_stats(stats[:, 2 * g + k, :], home[:, t, o:o + BANK]).then_inc(bn, 1)
                dve.wait_ge(bn, 4 * TILES * (b + 1))
                dve.sem_inc(bn_all, 1)
                nc.vector.bn_aggr(mean_var, stats[:].rearrange("p a n -> p (a n)")).then_inc(chain, 1)
                dve.wait_ge(gm_done, 2 * b + 1)
                nc.vector.tensor_tensor(dev, mean_var[:, 0:1], ps_small[:, 0:1], ALU.subtract).then_inc(chain, 1)
                dve.wait_ge(chain, 4 * b + 2)
                nc.vector.scalar_tensor_tensor(out=spread, in0=dev, scalar=dev, in1=mean_var[:, 1:2],
                                               op0=ALU.mult, op1=ALU.add).then_inc(chain, 1)
                dve.wait_ge(gm_done, 2 * b + 2)
                nc.vector.tensor_scalar(var_eps, ps_small[:, 1:2], EPS, None, ALU.add).then_inc(chain, 1)
                dve.wait_ge(rstd_done, b + 1)
                nc.vector.tensor_tensor(scale, rstd, params[:, 1:2], ALU.mult).then_inc(scaled, 1)
                dve.wait_ge(scaled, 3 * b + 1)
                nc.vector.tensor_tensor(shift0, scale, ps_small[:, 0:1], ALU.mult).then_inc(scaled, 1)
                dve.wait_ge(scaled, 3 * b + 2)
                nc.vector.tensor_tensor(shift, params[:, 2:3], shift0, ALU.subtract).then_inc(scaled, 1)
                dve.wait_ge(scaled, 3 * b + 3)

            for jj in range(JJ):
                low_parts(0, 0, jj)
            image(0, True, False)
            with dve.Fori(1, B - 1) as b:
                image(b, False, False)
            image(B - 1, False, True)
            for t in range(TILES):
                norm(t)

        @block.gpsimd
        def _(pool):
            for i in range(2):
                pool.wait_ge(m_out[i], 16 * (W_CHUNKS // 2))
            src = scratch.rearrange("(r b) k n -> r b k n", r=2)

            def fetch(b):
                if not at_start(b):
                    pool.wait_ge(permuted, 2 * JJ * b)
                for first in range(2):
                    for r in range(2):
                        part = src[(r + first) % 2, bass.ds(b, 1)].rearrange("a k n -> (a k) n")
                        pool.dma_start(raw[r * SLOTS:(r + 1) * SLOTS, first].rearrange("p o k -> p (o k)"),
                                       part).then_inc(raw_in, 16)

            def permute(b, jj):
                pool.wait_ge(raw_in, 64 * (b + 1))
                if not at_start(b):
                    pool.wait_ge(kh_done, JJ * SL * b - JJ + 1 + jj)
                pool.sem_inc(modes_free, 1)
                o = slice(jj * HC, (jj + 1) * HC)
                dst = modes[:, o, :].rearrange("p o (r k) -> p r o k", r=2)
                nc.gpsimd.tensor_copy(dst[:, 0], raw[:, 0, o]).then_inc(permuted, 1)
                nc.gpsimd.tensor_scalar(dst[:, 1], raw[:, 1, o], signs[C:P, 0:1], None, ALU.mult
                                        ).then_inc(permuted, 1)

            def root(b):
                pool.wait_ge(chain, 4 * b + 4)
                nc.gpsimd.tensor_tensor(rstd, var_eps, signs[:, 1:2], ALU.pow).then_inc(rstd_done, 1)

            fetch(0)
            for jj in range(JJ):
                permute(0, jj)
            with pool.Fori(0, B - 1) as b:
                fetch(b + 1)
                for jj in range(JJ):
                    permute(b + 1, jj)
                root(b)
            root(B - 1)


_INS = ["x", "L0_conv_w1_re", "L0_conv_w1_im", "L0_conv_w2_re", "L0_conv_w2_im", "L0_conv_conv_w",
        "L0_conv_conv_b", "L0_conv_gn_w", "L0_conv_gn_b"]


def kernel(**inputs):
    import concourse.bacc as _bacc
    from concourse.bass_utils import run_bass_kernel_spmd as _run

    nc = _bacc.Bacc("TRN2", target_bir_lowering=False, num_devices=1)
    arrays, args = {}, []
    for name in _INS:
        a = np.ascontiguousarray(inputs[name])
        arrays[f"in_{name}"] = a
        args.append(nc.dram_tensor(f"in_{name}", a.shape, F32, kind="ExternalInput").ap())
    arrays["in_constants"] = constants()
    args.append(nc.dram_tensor("in_constants", arrays["in_constants"].shape, F32, kind="ExternalInput").ap())
    args.append(nc.dram_tensor("out", (B, C, H, W), F32, kind="ExternalOutput").ap())
    fno_layer(nc, *args)
    r = _run(nc, [arrays], core_ids=[0])
    return r.results[0]["out"]
```

```python
from contextlib import ExitStack

import numpy as np

import concourse.bass as bass
from concourse import mybir

F32 = mybir.dt.float32
F32R = mybir.dt.float32r
ALU = mybir.AluOpType
ACT = mybir.ActivationFunctionType

B, C, H, W = 16, 64, 256, 256
MX, MY = 16, 16
GROUPS = 32
EPS = 1e-5
P = 128
HH = H // 2
KH = MX + 1
KC = KH + MX
SLOTS = 2 * MX
RI = 2
MODE = 2 * B

CH = 4
NX = 4
NF = 64
TILE = 2048
A_TILES = C // CH

WX = 8
W_CHUNKS = 2 * MX // WX
W_PLACE = (0, 1, 2, 0)
W_MODES = WX * MY // 8
MX_STORE = 4
STORES = 2 * MX // MX_STORE

TILES = HH * W // TILE
GRP = 1024
BANK = 512
GROUPS_B = HH * W // GRP
SL = 4
SL_ROWS = HH // SL
SL_TILES = TILES // SL
QUAD = 4
JJ = 2
LEAD = 2
NXB = NX * TILE // GRP
HC = C // JJ

CONST_COLS = {
    "dft_h": 2 * NF, "dft_w": 2 * 2 * 64, "idft_h": 256, "idft_w": 256, "group": P,
    "dup": P, "same_half": P, "ident": P, "sign": 1, "neg_half": 1,
}


def top12(a):
    u = np.asarray(a, np.float32).view(np.uint32).astype(np.uint64)
    u = (u + 0x7FF + ((u >> 12) & 1)) & 0xFFFFF000
    return u.astype(np.uint32).view(np.float32)


def at_start(n):
    return isinstance(n, int) and n <= 0


def constants():
    c = {}
    p = np.arange(P)
    k = np.arange(KH)
    dft_h = np.zeros((P, 2, NF))
    for r in range(2):
        angle = 2 * np.pi * ((2 * p + r)[:, None] * k[None, :] % H) / H
        dft_h[:, r, :KH] = np.cos(angle)
        dft_h[:, r, KH:KC] = np.sin(angle)[:, 1:]
    c["dft_h"] = dft_h
    dft_w = np.zeros((P, 2, 2, 2, RI, MY))
    for chunk in range(2):
        angle = 2 * np.pi * ((P * chunk + p)[:, None] * np.arange(MY)[None, :] % W) / W
        cos, sin = np.cos(angle), np.sin(angle)
        for sign, s in ((0, 1), (1, -1)):
            dft_w[:, chunk, 0, sign, 0] = cos
            dft_w[:, chunk, 0, sign, 1] = -sin
            dft_w[:, chunk, 1, sign, 0] = -s * sin
            dft_w[:, chunk, 1, sign, 1] = -s * cos
    c["dft_w"] = dft_w
    kh = np.concatenate([np.arange(MX), -1 - np.arange(MX)])
    h = (np.arange(HH)[:, None] + HH * np.arange(2)[None, :]).ravel()
    angle = 2 * np.pi * (kh[:, None] * h[None, :] % H) / H
    c["idft_h"] = np.concatenate([np.cos(angle), -np.sin(angle)])
    angle = 2 * np.pi * (np.arange(MY)[:, None] * np.arange(W)[None, :] % W) / W
    twice = np.where(np.arange(MY) > 0, 2.0, 1.0)[:, None] / (H * W)
    e = np.concatenate([twice * np.cos(angle), -twice * np.sin(angle)]).astype(np.float32)
    high = top12(e)
    low = top12(e - high)
    c["idft_w"] = np.concatenate([high, low, high, low])
    span = 2 * C // GROUPS
    c["group"] = (p[:, None] // span == p[None, :] // span) / span
    c["dup"] = np.zeros((P, P))
    c["dup"][:C] = np.arange(C)[:, None] == p[None, :] // 2
    c["same_half"] = p[:, None] % 2 == p[None, :] % 2
    c["ident"] = np.eye(P)
    c["sign"] = np.where(p % (2 * SLOTS) < SLOTS, 1.0, -1.0)
    c["neg_half"] = np.full(P, -0.5)
    return np.concatenate([np.asarray(c[n], np.float32).reshape(P, -1) if c[n].shape[0] == P else
                           np.pad(np.asarray(c[n], np.float32), ((0, P - c[n].shape[0]), (0, 0)))
                           for n in CONST_COLS], axis=1)


def fno_layer(nc, x, w1_re, w1_im, w2_re, w2_im, conv_w, conv_b, gn_w, gn_b, const, out):
    ctx = ExitStack()
    with ctx:
        def sb(name, shape, dt=F32, stack=ctx):
            return stack.enter_context(nc.sbuf_tensor(name, shape, dt))

        def psum(name, shape):
            return ctx.enter_context(nc.psum_tensor(name, shape, F32))

        def sem(name):
            return ctx.enter_context(nc.semaphore(name))

        x_tiles = sb("x_tiles", [P, NX, TILE])
        xs = [x_tiles[:, i, :] for i in range(NX)]
        xb = [xs[i // 2][:, i % 2 * GRP:(i % 2 + 1) * GRP] for i in range(NXB)]
        idft_h = sb("idft_h", [P, 256])
        idft_w = sb("idft_w", [P, 256], F32R)
        group = sb("group", [P, P])
        mix = sb("mix", [P, P])
        params = sb("params", [P, 3])
        signs = sb("signs", [P, 2])

        early = ExitStack()
        dft_h = sb("dft_h", [P, 2, NF], stack=early)
        dft_w = sb("dft_w", [P, 2, 2, 64], stack=early)
        sums = sb("sums", [P, 2, KC, C], stack=early)
        spec = sb("spec", [P, SLOTS, MY, MODE], stack=early)
        w0, w2 = (sb(f"weights{i}", [P, C, WX * MY], stack=early) for i in (0, 2))
        wts = [w0[:], x_tiles[:].rearrange("p t n -> p (t n)").rearrange("p (o k) -> p o k", o=C), w2[:]]
        mixed1 = sb("mixed1", [MODE, MX_STORE, C * MY], stack=early)
        mixed = [sums[0:MODE].rearrange("p w k c -> p (w k c)")[:, 0:MX_STORE * C * MY]
                 .rearrange("p (x n) -> p x n", x=MX_STORE), mixed1[:]]
        once = w2[:].rearrange("p a b -> p (a b)")
        dup = once[:, 0:P]
        same_half = once[:, P:2 * P]
        ident = once[:, 2 * P:3 * P]
        idft_w_raw = once[:, 3 * P:5 * P]
        cw = once[0:C, 5 * P:5 * P + C]
        cw2 = once[0:C, 6 * P:7 * P]
        prm = once[0:C, 7 * P:7 * P + 3]
        prod = once[:, 8 * P:9 * P]
        early.close()

        home = sb("home", [P, TILES, TILE])
        rows = [sb(f"row_modes{i}", [P, SL_ROWS, P], F32R) for i in range(2)]
        both = sb("modes", [P, C * RI * MY])
        modes = both[0:C].rearrange("p (o k) -> p o k", o=C)
        raw = both[C:P].rearrange("p (r o k) -> p r o k", r=RI, o=C)
        stats = sb("stats", [P, TILES * 4, 6])
        small = sb("small", [P, 12])
        mean_var, dev, spread = small[:, 0:2], small[:, 2:3], small[:, 3:4]
        var_eps, rstd, scale, shift = (small[:, i:i + 1] for i in range(4, 8))

        scratch = nc.dram_tensor("mixed_modes", [RI * B, SLOTS, C * MY], F32).ap()

        ps_main = psum("ps_main", [P, 4, BANK])
        ps_slice = psum("ps_slice", [P, 2, BANK])
        ps_small = psum("ps_small", [P, BANK])

        dft_in = sem("dft_in")
        const_in = sem("const_in")
        cw_ready = sem("cw_ready")
        setup_mm = sem("setup_mm")
        mask_done = sem("mask_done")
        setup_done = sem("setup_done")
        x_in = [sem(f"x_in{i}") for i in range(NX)]
        xb_in = [sem(f"xb_in{i}") for i in range(NXB)]
        w_in = [sem(f"w_in{i}") for i in range(3)]
        a_sums = sem("a_sums")
        a_copied = sem("a_copied")
        a_modes = sem("a_modes")
        a_kept = sem("a_kept")
        m_mixed = sem("m_mixed")
        m_even = sem("m_even")
        m_odd = sem("m_odd")
        m_out = [sem(f"m_out{i}") for i in range(2)]
        raw_in = sem("raw_in")
        permuted = sem("permuted")
        kh_done = sem("kh_done")
        high = sem("high")
        low = sem("low")
        low2 = sem("low2")
        pre = sem("pre")
        gelu = sem("gelu")
        bn = sem("bn")
        bn_all = sem("bn_all")
        first_real = sem("first_real")
        first_imag = sem("first_imag")
        modes_free = sem("modes_free")
        chain = sem("chain")
        scaled = sem("scaled")
        gm_done = sem("gm_done")
        rstd_done = sem("rstd_done")
        normed = sem("normed")
        stored = [sem(f"stored{i}") for i in range(TILES)]
        stored_first = sem("stored_first")

        x_a = x.rearrange("b c (p r) w -> p (b c) (r w)", r=2)
        x_b = x.rearrange("b c h w -> b (c h w)").rearrange("b (p n) -> p b n", p=P)
        out_b = out.rearrange("b c h w -> b (c h w)").rearrange("b (p n) -> p b n", p=P)
        col = {}
        at = 0
        for n, k in CONST_COLS.items():
            col[n] = const[:, at:at + k]
            at += k

        n_const = 12
        m_bank = [ps_slice[0:MODE, 0, :], ps_slice[0:MODE, 1, :], ps_main[0:MODE, 3, :], ps_main[0:MODE, 2, :]]

        block = ctx.enter_context(nc.Block())

        @block.sync
        def _(sp):
            sp.dma_start(dft_h[:].rearrange("p a b -> p (a b)"), col["dft_h"]).then_inc(dft_in, 16)
            for s in range(NX):
                sp.dma_start(xs[s].rearrange("p (c n) -> p c n", c=CH),
                             x_a[:, s * CH:(s + 1) * CH, :]).then_inc(x_in[s], 16)
            sp.dma_start(dft_w[:].rearrange("p a b c -> p (a b c)"), col["dft_w"]).then_inc(const_in, 16)
            sp.dma_start(idft_h[:], col["idft_h"]).then_inc(const_in, 16)
            sp.dma_start(idft_w_raw, col["idft_w"]).then_inc(const_in, 16)
            sp.dma_start(group[:], col["group"]).then_inc(const_in, 16)
            sp.dma_start(dup, col["dup"]).then_inc(const_in, 16)
            sp.dma_start(same_half, col["same_half"]).then_inc(const_in, 16)
            sp.dma_start(ident, col["ident"]).then_inc(const_in, 16)
            sp.dma_start(signs[:], const[:, at - 2:at]).then_inc(const_in, 16)
            sp.dma_start(cw, conv_w).then_inc(const_in, 16)
            for i, v in enumerate((conv_b, gn_w, gn_b)):
                sp.dma_start(prm[:, i:i + 1], v.rearrange("(c a) -> c a", a=1)).then_inc(const_in, 16)

            def weights(j, half):
                xx = WX * (j % (W_CHUNKS // 2))
                w = ((w1_re, w1_im) if j < W_CHUNKS // 2 else (w2_re, w2_im))[half]
                place = W_PLACE[j]
                sp.dma_start(wts[place][half * C:(half + 1) * C],
                             w[:, :, xx:xx + WX, :].rearrange("i o x y -> i o (x y)")
                             ).then_inc(w_in[place], 16)

            loads = B * A_TILES // NX
            between = [None, (0, 0), (0, 1), (2, 0), (2, 1)]
            for i, chunk_half in enumerate(between):
                if chunk_half == (2, 0):
                    sp.wait_ge(setup_done, 5)
                if chunk_half:
                    weights(*chunk_half)
                with sp.Fori(max(loads * i // len(between), 1), loads * (i + 1) // len(between)) as u:
                    for s in range(NX):
                        sp.wait_ge(a_sums, (u - 1) * NX + s + 1)
                        sp.dma_start(xs[s].rearrange("p (c n) -> p c n", c=CH),
                                     x_a[:, bass.ds((u * NX + s) * CH, CH), :]).then_inc(x_in[s], 16)

            def fetch(b, g):
                sp.dma_start(xb[g % NXB], x_b[:, bass.ds(b, 1), g * GRP:(g + 1) * GRP]
                             .rearrange("p a n -> p (a n)")).then_inc(xb_in[g % NXB], 16)

            sp.wait_ge(a_sums, B * A_TILES)
            for half in range(2):
                weights(1, half)
            for j in range(STORES):
                sp.wait_ge(m_even, (j + 1) * 4)
                sp.wait_ge(m_odd, (j + 1) * 4)
                first = MX_STORE * j if j < STORES // 2 else SLOTS - MX_STORE * (j - STORES // 2 + 1)
                sp.dma_start(scratch[:, first:first + MX_STORE, :], mixed[j % 2]).then_inc(m_out[j % 2], 16)
                if j == 1:
                    sp.wait_ge(m_mixed, W_MODES)
                    for half in range(2):
                        weights(3, half)
                if 3 <= j < 7:
                    if j == 3:
                        sp.wait_ge(m_mixed, 2 * W_MODES)
                    for g in (2 * (j - 3), 2 * (j - 3) + 1):
                        fetch(0, g)

            def fetch_modes(b):
                src = scratch.rearrange("(r b) k n -> r b k n", r=2)
                for first in range(2):
                    for r in range(2):
                        part = src[(r + first) % 2, bass.ds(b, 1)].rearrange("a k n -> (a k) n")
                        sp.dma_start(raw[r * SLOTS:(r + 1) * SLOTS, first].rearrange("p o k -> p (o k)"),
                                     part).then_inc(raw_in, 16)

            for i in range(2):
                sp.wait_ge(m_out[i], 16 * (STORES // 2))
            fetch_modes(0)

            def load(b, g):
                sp.wait_ge(pre, GROUPS_B * b + g - NXB + 1)
                fetch(b, g)

            def store(b, t):
                for o, end in ((0, GRP), (GRP, TILE)) if t == 0 else ((0, TILE),):
                    sp.wait_ge(normed, (TILES + 1) * b + (t + 1 if end == TILE else 0) + 1)
                    sp.dma_start(out_b[:, bass.ds(b, 1), t * TILE + o:t * TILE + end]
                                 .rearrange("p a n -> p (a n)"), home[:, t, o:end]
                                 ).then_inc(stored[t] if end == TILE else stored_first, 16)

            for g in range(NXB, GROUPS_B):
                load(0, g)
                if g == NXB + 4:
                    sp.wait_ge(permuted, 2 * JJ)
                    fetch_modes(1)

            def stores_and_loads(b, more):
                for g in range(NXB):
                    load(b + 1, g)
                if more:
                    sp.wait_ge(permuted, 2 * JJ * (b + 2))
                    fetch_modes(b + 2)
                load(b + 1, NXB)
                for t in range(LEAD):
                    store(b, t)
                for g in range(NXB + 1, GROUPS_B):
                    load(b + 1, g)
                    if g % 2:
                        store(b, LEAD + (g - NXB) // 2)
                for t in range(LEAD + (GROUPS_B - NXB) // 2, TILES):
                    store(b, t)

            with sp.Fori(0, B - 2) as b:
                stores_and_loads(b, True)
            stores_and_loads(B - 2, False)
            for t in range(TILES):
                store(B - 1, t)
            for done in [stored_first] + stored:
                sp.wait_ge(done, 16 * B)

        @block.tensor
        def _(pe):
            pe.sem_inc(a_modes, 1)
            def sums_over_h(q, slots):
                for s in slots:
                    pe.wait_ge(x_in[s], (q + 1) * 16)
                    pe.wait_ge(a_copied, q * NX + s + 1)
                    ps = ps_slice[:, s % 2, 0:CH * 2 * NF].rearrange("p (c w k) -> p c w k", c=CH, w=2)
                    for c in range(CH):
                        for w in range(2):
                            for r in range(2):
                                o = c * 512 + r * W + w * P
                                mm = pe.matmul(ps[:, c, w, :], xs[s][:, o:o + P], dft_h[:, r, :],
                                               start=(r == 0), stop=(r == 1))
                    mm.then_inc(a_sums, 1)

            def sums_over_w(b):
                pe.wait_ge(a_copied, (b + 1) * A_TILES + 2)
                pe.wait_ge(a_kept, b * 8 + 1)
                for k in range(KH):
                    ps = ps_main[0:C, k // 8, k % 8 * 64:k % 8 * 64 + 64]
                    terms = [(w, t) for t in range(2 if k else 1) for w in range(2)]
                    for n, (w, t) in enumerate(terms):
                        mm = pe.matmul(ps, sums[:, w, k + t * MX, :], dft_w[:, w, t, :],
                                       start=(n == 0), stop=(n == len(terms) - 1))
                mm.then_inc(a_modes, 1)

            pe.wait_ge(dft_in, 16)
            sums_over_h(0, range(NX))
            pe.wait_ge(const_in, 16 * n_const)
            pe.wait_ge(cw_ready, 1)
            pe.matmul(ps_main[:, 0, 0:P], cw2, dup[0:C, :], start=True, stop=True).then_inc(setup_mm, 1)
            pe.matmul(ps_main[:, 1, 0:3], dup[0:C, :], prm, start=True, stop=True).then_inc(setup_mm, 1)
            quads = A_TILES // NX
            with pe.Fori(1, quads) as q:
                sums_over_h(q, range(NX))
            pe.wait_ge(setup_done, 5)
            with pe.Fori(1, B) as b:
                sums_over_h(b * quads, (0,))
                sums_over_w(b - 1)
                sums_over_h(b * quads, range(1, NX))
                with pe.Fori(1, quads) as q:
                    sums_over_h(b * quads + q, range(NX))
            sums_over_w(B - 1)

            pe.wait_ge(a_kept, B * 8 + 1 - 4)
            for j in range(W_CHUNKS):
                pe.wait_ge(w_in[W_PLACE[j]], 64 if j == W_CHUNKS - 1 else 32)
                for xx in range(WX):
                    slot = WX * j + xx if j < W_CHUNKS // 2 else SLOTS - 1 - (WX * (j - W_CHUNKS // 2) + xx)
                    for half in range(2):
                        g = W_MODES * j + 2 * xx + half
                        if g == 3:
                            pe.wait_ge(a_kept, B * 8 + 1)
                        if g >= 4:
                            pe.wait_ge(m_even if g % 2 == 0 else m_odd, (g - 4) // 2 + 1)
                        for y in range(8):
                            ky = 8 * half + y
                            mm = pe.matmul(m_bank[g % 4][:, y * C:(y + 1) * C],
                                           spec[:, slot, ky, :], wts[W_PLACE[j]][:, :, xx * MY + ky],
                                           start=True, stop=True)
                        mm.then_inc(m_mixed, 1)

            def kh_inverse(b, sl, jj):
                n = JJ * (SL * b + sl) + jj
                if not at_start(n - 1):
                    pe.wait_ge(low, QUAD * (n - 1))
                if at_start(n - JJ + 1):
                    pe.wait_ge(first_real, jj + 1)
                    pe.wait_ge(first_imag, jj + 1)
                elif sl == 0:
                    pe.wait_ge(permuted, 2 * (JJ * b + jj + 1))
                for i in range(8):
                    o = QUAD * (8 * jj + i)
                    w = modes[:, o:o + QUAD, :].rearrange("p o k -> p (o k)")
                    mm = pe.matmul(ps_slice[:, jj, i * 64:(i + 1) * 64], w,
                                   idft_h[0:C, sl * 64:(sl + 1) * 64], start=True, stop=True)
                mm.then_inc(kh_done, 1)

            def group_means(b):
                pe.wait_ge(chain, 4 * b + 1)
                pe.matmul(ps_small[:, 0:1], group[:], mean_var[:, 0:1], start=True, stop=True
                          ).then_inc(gm_done, 1)
                pe.wait_ge(chain, 4 * b + 3)
                pe.matmul(ps_small[:, 1:2], group[:], spread, start=True, stop=True).then_inc(gm_done, 1)

            def pixels(b, groups):
                for g in groups:
                    sl = g // (2 * SL_TILES)
                    if g % (2 * SL_TILES) == 0:
                        pe.wait_ge(low2, JJ * (SL * b + sl + 1))
                    pe.wait_ge(xb_in[g % NXB], 16 * (GROUPS_B // NXB * b + g // NXB + 1))
                    if not at_start(GROUPS_B * b + g - 1):
                        pe.wait_ge(gelu, GROUPS_B * b + g - 1)
                    for k in range(2):
                        o = k * BANK
                        bank = ps_main[:, 2 * (g % 2) + k, :]
                        pe.matmul(bank, mix[:], xb[g % NXB][:, o:o + BANK], start=True, stop=True,
                                  skip_group_check=True)
                        for r in range(2):
                            row = (g * GRP + o) // W + r - sl * SL_ROWS
                            mm = pe.matmul(bank[:, r * W:(r + 1) * W], rows[sl % 2][:, row, :],
                                           idft_w[:], start=False, stop=True,
                                           skip_group_check=True)
                    mm.then_inc(pre, 1)

            def image(b, first, last):
                for t in range(TILES):
                    nxt = t // SL_TILES + 1
                    if t == 0 and not first:
                        pixels(b, (0,))
                        group_means(b - 1)
                    if t % 2 == 0 and not (last and nxt == SL):
                        kh_inverse(b + nxt // SL, nxt % SL, t % SL_TILES // 2)
                    pixels(b, (1,) if t == 0 and not first else (2 * t, 2 * t + 1))

            for jj in range(JJ):
                kh_inverse(0, 0, jj)
            image(0, True, False)
            with pe.Fori(1, B - 1) as b:
                image(b, False, False)
            image(B - 1, False, True)
            group_means(B - 1)

        @block.scalar
        def _(act):
            act.sem_inc(a_copied, 2)

            def keep_sums(b, q):
                for s in range(NX):
                    act.wait_ge(a_sums, b * A_TILES + q * NX + s + 1)
                    ps = ps_slice[:, s % 2, 0:CH * 2 * NF].rearrange("p (c w k) -> p w k c", c=CH, w=2)[:, :, 0:KC]
                    nc.scalar.copy(sums[:, :, :, bass.ds((q * NX + s) * CH, CH)], ps
                                   ).then_inc(a_copied, 1)

            keep_sums(0, 0)
            act.wait_ge(setup_mm, 2)
            nc.scalar.copy(params[:], ps_main[:, 1, 0:3]).then_inc(setup_done, 1)
            nc.scalar.copy(idft_w[:], idft_w_raw).then_inc(setup_done, 1)
            with act.Fori(1, A_TILES // NX) as q:
                keep_sums(0, q)
            with act.Fori(1, B) as b:
                act.wait_ge(a_modes, b + 1)
                with act.Fori(0, A_TILES // NX) as q:
                    keep_sums(b, q)

            def keep(g, engine_copy, done):
                j, xx, half = g // 8, g // 2 % MX_STORE, g % 2
                place = xx if j < STORES // 2 else MX_STORE - 1 - xx
                dst = mixed[j % 2][:, place, :].rearrange("p (o k) -> p o k", k=MY)[:, :, 8 * half:8 * half + 8]
                engine_copy(dst, m_bank[g % 4].rearrange("p (k o) -> p o k", o=C)
                            ).then_inc(done, 1)

            for g in range(0, 8 * STORES, 2):
                act.wait_ge(m_mixed, g + 1)
                if g % 8 == 0 and g >= 16:
                    act.wait_ge(m_out[g // 8 % 2], 16 * (g // 16))
                keep(g, nc.scalar.copy, m_even)

            def high_parts(b, sl, jj):
                n = JJ * (SL * b + sl) + jj
                act.wait_ge(kh_done, n + 1)
                if jj == 0 and not at_start(SL * b + sl - 1):
                    act.wait_ge(pre, 8 * (SL * b + sl - 1))
                for q in range(QUAD):
                    for copy in range(2):
                        dst = rows[sl % 2][32 * copy:32 * copy + 32].rearrange(
                            "p r (j q s) -> p j q r s", q=QUAD, s=2)[:, 8 * jj:8 * jj + 8, q]
                        src = ps_slice[32 * q:32 * q + 32, jj, :].rearrange("p (j r s) -> p j r s", j=8, s=2)
                        part = nc.scalar.copy(dst, src)
                    part.then_inc(high, 1)

            def low_again(b, sl, jj):
                n = JJ * (SL * b + sl) + jj
                act.wait_ge(low, QUAD * (n + 1))
                part = [rows[sl % 2][32 * i:32 * i + 32, :, 64 * jj:64 * jj + 64] for i in (2, 3)]
                nc.scalar.copy(part[1], part[0].bitcast(F32)).then_inc(low2, 1)

            def image(b, last):
                for t in range(TILES):
                    nxt = t // SL_TILES + 1
                    if not (last and nxt == SL):
                        step = high_parts if t % 2 == 0 else low_again
                        step(b + nxt // SL, nxt % SL, t % SL_TILES // 2)
                    for g in (2 * t, 2 * t + 1):
                        if not at_start(b) and (g < 2 or g % 2 == 0):
                            act.wait_ge(stored_first if g == 0 else stored[t], 16 * b)
                        act.wait_ge(pre, GROUPS_B * b + g + 1)
                        o = g % 2 * GRP
                        nc.scalar.activation(home[:, t, o:o + GRP],
                                             ps_main[:, 2 * (g % 2):2 * (g % 2) + 2, :].rearrange("p a n -> p (a n)"),
                                             ACT.Gelu, bias=params[:, 0:1]).then_inc(gelu, 1)

            act.wait_ge(setup_done, 5)
            act.wait_ge(raw_in, 64)
            for jj in range(JJ):
                o = slice(jj * HC, (jj + 1) * HC)
                nc.scalar.copy(modes[:, o, 0:MY], raw[:, 0, o]).then_inc(first_real, 1)
            for jj in range(JJ):
                high_parts(0, 0, jj)
            image(0, False)
            with act.Fori(1, B - 1) as b:
                image(b, False)
            image(B - 1, True)

        @block.vector
        def _(dve):
            dve.sem_inc(a_kept, 1)
            dve.wait_ge(const_in, 16 * n_const)
            nc.vector.tensor_copy(cw2.rearrange("p (c s) -> p c s", s=2),
                                  cw.unsqueeze(2).broadcast_to([C, C, 2])).then_inc(cw_ready, 1)
            dve.wait_ge(setup_mm, 2)
            nc.vector.tensor_tensor(prod, ps_main[:, 0, 0:P], same_half, ALU.mult).then_inc(mask_done, 1)
            dve.wait_ge(mask_done, 1)
            nc.vector.tensor_tensor(mix[:], prod, ident, ALU.add).then_inc(setup_done, 3)

            with dve.Fori(0, B) as b:
                dve.wait_ge(a_modes, b + 2)
                ps = ps_main[0:C, 0:3, :].rearrange("p a n -> p (a n)")[:, 0:KH * 64]
                ps = ps.rearrange("p (k g r y) -> p k g r y", g=2, r=2, y=MY)
                for sign in range(2):
                    src = ps[:, sign:sign + MX, sign]
                    for half in range(2):
                        dst = spec[half * C:(half + 1) * C, sign * MX:(sign + 1) * MX]
                        dst = dst.rearrange("p k y (r b) -> p k r y b", r=2)
                        for r in range(2):
                            d = dst[:, :, r, :, bass.ds(b, 1)].rearrange("p k y a -> p k (y a)")
                            if half == 0:
                                nc.vector.tensor_copy(d, src[:, :, r]).then_inc(a_kept, 1)
                            elif r == 0:
                                nc.vector.tensor_scalar(d, src[:, :, 1], -1.0, None, ALU.mult
                                                        ).then_inc(a_kept, 1)
                            else:
                                nc.vector.tensor_copy(d, src[:, :, 0]).then_inc(a_kept, 1)

            for g in range(1, 8 * STORES, 2):
                j, xx = g // 8, g // 2 % MX_STORE
                dve.wait_ge(m_mixed, g + 1)
                if g % 8 == 1 and g >= 16:
                    dve.wait_ge(m_out[j % 2], 16 * (j // 2))
                place = xx if j < STORES // 2 else MX_STORE - 1 - xx
                dst = mixed[j % 2][:, place, :].rearrange("p (o k) -> p o k", k=MY)[:, :, 8:16]
                nc.vector.tensor_copy(dst, m_bank[g % 4].rearrange("p (k o) -> p o k", o=C)
                                      ).then_inc(m_odd, 1)

            def low_parts(b, sl, jj):
                n = JJ * (SL * b + sl) + jj
                for q in range(QUAD):
                    dve.wait_ge(high, QUAD * n + q + 1)
                    part = [rows[sl % 2][32 * i:32 * i + 32].rearrange("p r (j q s) -> p j q r s", q=QUAD, s=2)
                            [:, 8 * jj:8 * jj + 8, q] for i in (0, 2)]
                    src = ps_slice[32 * q:32 * q + 32, jj, :].rearrange("p (j r s) -> p j r s", j=8, s=2)
                    nc.vector.tensor_tensor(part[1], src, part[0].bitcast(F32), ALU.subtract).then_inc(low, 1)

            def norm(t):
                for o, end in ((0, GRP), (GRP, TILE)) if t == 0 else ((0, TILE),):
                    nc.vector.tensor_scalar(home[:, t, o:end], home[:, t, o:end], scale, shift,
                                            ALU.mult, ALU.subtract).then_inc(normed, 1)

            def image(b, first, last):
                if not first:
                    for t in range(LEAD):
                        norm(t)
                for t in range(TILES):
                    if not first:
                        for o in range(LEAD + 2 * t, min(LEAD + 2 * t + 2, TILES)):
                            norm(o)
                    nxt = t // SL_TILES + 1
                    if t % 2 == 0 and not (last and nxt == SL):
                        low_parts(b + nxt // SL, nxt % SL, t % SL_TILES // 2)
                    for g in (2 * t, 2 * t + 1):
                        dve.wait_ge(gelu, GROUPS_B * b + g + 1)
                        for k in range(2):
                            o = g % 2 * GRP + k * BANK
                            nc.vector.bn_stats(stats[:, 2 * g + k, :], home[:, t, o:o + BANK]).then_inc(bn, 1)
                dve.wait_ge(bn, 4 * TILES * (b + 1))
                dve.sem_inc(bn_all, 1)
                nc.vector.bn_aggr(mean_var, stats[:].rearrange("p a n -> p (a n)")).then_inc(chain, 1)
                dve.wait_ge(gm_done, 2 * b + 1)
                nc.vector.tensor_tensor(dev, mean_var[:, 0:1], ps_small[:, 0:1], ALU.subtract).then_inc(chain, 1)
                dve.wait_ge(chain, 4 * b + 2)
                nc.vector.scalar_tensor_tensor(out=spread, in0=dev, scalar=dev, in1=mean_var[:, 1:2],
                                               op0=ALU.mult, op1=ALU.add).then_inc(chain, 1)
                dve.wait_ge(gm_done, 2 * b + 2)
                nc.vector.tensor_scalar(var_eps, ps_small[:, 1:2], EPS, None, ALU.add).then_inc(chain, 1)
                dve.wait_ge(rstd_done, b + 1)
                nc.vector.tensor_tensor(scale, rstd, params[:, 1:2], ALU.mult).then_inc(scaled, 1)
                dve.wait_ge(scaled, 2 * b + 1)
                nc.vector.scalar_tensor_tensor(out=shift, in0=scale, scalar=ps_small[:, 0:1], in1=params[:, 2:3],
                                               op0=ALU.mult, op1=ALU.subtract).then_inc(scaled, 1)
                dve.wait_ge(scaled, 2 * b + 2)

            dve.wait_ge(raw_in, 64)
            for jj in range(JJ):
                o = slice(jj * HC, (jj + 1) * HC)
                nc.vector.tensor_scalar(modes[:, o, MY:2 * MY], raw[:, 1, o], signs[C:P, 0:1], None, ALU.mult
                                        ).then_inc(first_imag, 1)
            for jj in range(JJ):
                low_parts(0, 0, jj)
                dve.wait_ge(low, QUAD * (jj + 1))
                part = [rows[0][32 * i:32 * i + 32, :, 64 * jj:64 * jj + 64] for i in (2, 3)]
                nc.vector.tensor_copy(part[1], part[0].bitcast(F32)).then_inc(low2, 1)
            image(0, True, False)
            with dve.Fori(1, B - 1) as b:
                image(b, False, False)
            image(B - 1, False, True)
            for t in range(TILES):
                norm(t)

        @block.gpsimd
        def _(pool):
            def permute(b, jj):
                pool.wait_ge(raw_in, 64 * (b + 1))
                if not at_start(b):
                    pool.wait_ge(kh_done, JJ * SL * b - JJ + 1 + jj)
                pool.sem_inc(modes_free, 1)
                o = slice(jj * HC, (jj + 1) * HC)
                dst = modes[:, o, :].rearrange("p o (r k) -> p r o k", r=2)
                nc.gpsimd.tensor_copy(dst[:, 0], raw[:, 0, o]).then_inc(permuted, 1)
                nc.gpsimd.tensor_scalar(dst[:, 1], raw[:, 1, o], signs[C:P, 0:1], None, ALU.mult
                                        ).then_inc(permuted, 1)

            def root(b):
                pool.wait_ge(chain, 4 * b + 4)
                nc.gpsimd.tensor_tensor(rstd, var_eps, signs[:, 1:2], ALU.pow).then_inc(rstd_done, 1)

            pool.wait_ge(first_real, JJ)
            pool.wait_ge(first_imag, JJ)
            pool.sem_inc(permuted, 2 * JJ)
            with pool.Fori(0, B - 1) as b:
                for jj in range(JJ):
                    permute(b + 1, jj)
                root(b)
            root(B - 1)


_INS = ["x", "L0_conv_w1_re", "L0_conv_w1_im", "L0_conv_w2_re", "L0_conv_w2_im", "L0_conv_conv_w",
        "L0_conv_conv_b", "L0_conv_gn_w", "L0_conv_gn_b"]


def kernel(**inputs):
    import concourse.bacc as _bacc
    from concourse.bass_utils import run_bass_kernel_spmd as _run

    nc = _bacc.Bacc("TRN2", target_bir_lowering=False, num_devices=1)
    arrays, args = {}, []
    for name in _INS:
        a = np.ascontiguousarray(inputs[name])
        arrays[f"in_{name}"] = a
        args.append(nc.dram_tensor(f"in_{name}", a.shape, F32, kind="ExternalInput").ap())
    arrays["in_constants"] = constants()
    args.append(nc.dram_tensor("in_constants", arrays["in_constants"].shape, F32, kind="ExternalInput").ap())
    args.append(nc.dram_tensor("out", (B, C, H, W), F32, kind="ExternalOutput").ap())
    fno_layer(nc, *args)
    r = _run(nc, [arrays], core_ids=[0])
    return r.results[0]["out"]
```
